# Optimizing a Trainium2 kernel written in Bass

```python
import numpy as np
import jax
import jax.numpy as jnp

def _softmax(x, axis=-1):
    return jax.nn.softmax(x, axis=axis)

def _gelu(x):
    return jax.nn.gelu(x, approximate=True)

def _silu(x):
    return jax.nn.silu(x)

def _sigmoid(x):
    return jax.nn.sigmoid(x)

def _layernorm(x, axis=-1, eps=1e-05):
    m = jnp.mean(x, axis=axis, keepdims=True)
    v = jnp.var(x, axis=axis, keepdims=True)
    return (x - m) / jnp.sqrt(v + eps)

def _scatter_add(tgt, idx, src, axis=0):
    return tgt.at[idx].add(src)

def _segment_sum(src, seg, n):
    return jax.ops.segment_sum(src, seg, n)
kernel_name = 'mk_decoder_preln_d2_seqx_r4_198aec'

def setup_inputs(seed: int=0):
    np.random.seed(seed)
    _w = jnp.asarray

    def _rec_inputs():
        import jax
        import jax.numpy as jnp
        _rk = jax.random.key(seed)
        x = 7.22e-05 + 1 * jax.random.normal(jax.random.fold_in(_rk, 1), (16, 256, 256), jnp.float32)
        _lenS = 256 - jax.random.randint(jax.random.fold_in(_rk, 7), (16,), 0, max(1, 256 // 4) + 1, jnp.int32)
        _lenS2 = 256 - jax.random.randint(jax.random.fold_in(_rk, 8), (16,), 0, max(1, 256 // 4) + 1, jnp.int32)
        _ctx_1024P = jax.random.normal(jax.random.fold_in(_rk, 11), (16, 16, 256), jnp.float32)
        _ctx_1024c = jax.random.dirichlet(jax.random.fold_in(_rk, 511), 0.3 * jnp.ones((16,), jnp.float32), (16, 256))
        _ctx_1024t = jnp.einsum('bsk,bkd->bsd', _ctx_1024c, _ctx_1024P)
        _ctx_1024t = _ctx_1024t * jax.lax.rsqrt(jnp.mean(jnp.square(_ctx_1024t)) + 1e-12) * 0.953939
        ctx_1024 = 4.13588e-05 + 0.999923 * (_ctx_1024t + 0.3 * jax.random.normal(jax.random.fold_in(_rk, 611), (16, 256, 256), jnp.float32))
        fside_BxSxS_0 = 4.13588e-05 + 0.999923 * jax.random.normal(jax.random.fold_in(_rk, 13), (16, 256, 256), jnp.float32)
        _validS = jnp.arange(256)[None, :] < _lenS[:, None]
        _validS2 = jnp.arange(256)[None, :] < _lenS2[:, None]
        _causal = jnp.tril(jnp.ones((256, 256), dtype=bool))
        mask_Bx1x1xS2_ik0 = jnp.where(jnp.broadcast_to(_validS2[:, None, None, :], (16, 1, 1, 256)), 0, 1).astype(jnp.int32)
        mask_Bx16xSxS_bk1 = jnp.broadcast_to(_validS[:, None, None, :], (16, 16, 256, 256))
        return (x, ctx_1024, fside_BxSxS_0, mask_Bx1x1xS2_ik0, mask_Bx16xSxS_bk1)
    x, ctx_1024, fside_BxSxS_0, mask_Bx1x1xS2_ik0, mask_Bx16xSxS_bk1 = _rec_inputs()

    def _L0_attn_setup():
        import jax, jax.numpy as jnp
        import numpy as np
        D_MODEL = 256
        N_HEADS = 16
        HEAD_DIM = D_MODEL // N_HEADS
        CHUNK = 128
        B, T = (2, 512)

        def _chunked_causal_attention(q, k, v, cs):
            Bq, H, Tq, D = q.shape
            n = Tq // cs
            inv_sqrt_d = 1.0 / D ** 0.5
            qc = jnp.moveaxis(q.reshape(Bq, H, n, cs, D), 2, 0)
            kc = jnp.moveaxis(k.reshape(Bq, H, n, cs, D), 2, 0)
            vc = jnp.moveaxis(v.reshape(Bq, H, n, cs, D), 2, 0)
            ar = jnp.arange(cs)

            def per_q(qi, qb):
                q_idx = qi * cs + ar

                def step(carry, kv):
                    m, l, o = carry
                    ki, kb, vb = kv
                    s = jnp.einsum('bhqd,bhkd->bhqk', qb, kb) * inv_sqrt_d
                    k_idx = ki * cs + ar
                    causal = q_idx[:, None] >= k_idx[None, :]
                    s = jnp.where(causal, s, -jnp.inf)
                    s_max = jnp.max(s, axis=-1, keepdims=True)
                    m_new = jnp.maximum(m, s_max)
                    m_safe = jnp.where(jnp.isneginf(m_new), 0.0, m_new)
                    alpha = jnp.exp(m - m_safe)
                    p = jnp.exp(s - m_safe)
                    o = o * alpha + jnp.einsum('bhqk,bhkd->bhqd', p, vb)
                    l = l * alpha + jnp.sum(p, axis=-1, keepdims=True)
                    return ((m_new, l, o), None)
                init = (jnp.full((Bq, H, cs, 1), -jnp.inf, dtype=jnp.float32), jnp.zeros((Bq, H, cs, 1), dtype=jnp.float32), jnp.zeros_like(qb))
                (m, l, o), _ = jax.lax.scan(step, init, (jnp.arange(n), kc, vc))
                return o / jnp.maximum(l, 1e-09)
            out = jax.vmap(per_q)(jnp.arange(n), qc)
            return jnp.moveaxis(out, 0, 2).reshape(Bq, H, Tq, D)
        key = jax.random.key(seed)
        ks = jax.random.split(key, 5)
        x = jax.random.normal(ks[0], (B, T, D_MODEL), dtype=jnp.float32)
        mk = lambda k: jax.random.normal(k, (D_MODEL, D_MODEL), dtype=jnp.float32) * 0.02
        return {'x': x, 'Wq': mk(ks[1]), 'Wk': mk(ks[2]), 'Wv': mk(ks[3]), 'Wo': mk(ks[4])}
    _L0_attn_all = _L0_attn_setup()
    _L0_attn_in = {k: v for k, v in _L0_attn_all.items() if k in ('Wq', 'Wk', 'Wv', 'Wo')}
    del _L0_attn_all

    def _L0_xattn_setup():
        import jax, jax.numpy as jnp
        import numpy as np
        D_MODEL = 256
        N_HEADS = 16
        HEAD_DIM = D_MODEL // N_HEADS
        B, S = (4, 512)
        NEG = -1000000000.0

        def _split_heads(x):
            b, s, _ = x.shape
            return x.reshape(b, s, N_HEADS, HEAD_DIM).transpose(0, 2, 1, 3)
        key = jax.random.key(seed)
        ks = jax.random.split(key, 13)
        sc = 1.0 / np.sqrt(D_MODEL)
        return {'query': jax.random.normal(ks[0], (B, S, D_MODEL), jnp.float32), 'key': jax.random.normal(ks[1], (B, S, D_MODEL), jnp.float32), 'value': jax.random.normal(ks[2], (B, S, D_MODEL), jnp.float32), 'mask': jax.random.randint(ks[3], (B, 1, 1, S), 0, 2, jnp.int32), 'Wq': jax.random.normal(ks[4], (D_MODEL, D_MODEL), jnp.float32) * sc, 'bq': jax.random.normal(ks[5], (D_MODEL,), jnp.float32) * sc, 'Wk': jax.random.normal(ks[6], (D_MODEL, D_MODEL), jnp.float32) * sc, 'bk': jax.random.normal(ks[7], (D_MODEL,), jnp.float32) * sc, 'Wv': jax.random.normal(ks[8], (D_MODEL, D_MODEL), jnp.float32) * sc, 'bv': jax.random.normal(ks[9], (D_MODEL,), jnp.float32) * sc, 'Wo': jax.random.normal(ks[10], (D_MODEL, D_MODEL), jnp.float32) * sc, 'bo': jax.random.normal(ks[11], (D_MODEL,), jnp.float32) * sc}
    _L0_xattn_all = _L0_xattn_setup()
    _L0_xattn_in = {k: v for k, v in _L0_xattn_all.items() if k in ('Wq', 'bq', 'Wk', 'bk', 'Wv', 'bv', 'Wo', 'bo')}
    del _L0_xattn_all

    def _L0_ffn_setup():
        import jax, jax.numpy as jnp
        import numpy as np
        N_GROUP = 8
        TOPK_GROUP = 4
        TOPK = 8
        ROUTED_SCALE = 2.5
        B, S, D, F, E = (4, 512, 256, 128, 64)

        def _route(x, w_router, b_router):
            scores = jax.nn.sigmoid(jnp.einsum('bsd,de->bse', x, w_router)).astype(jnp.float32)
            swb = scores + b_router
            e = scores.shape[-1]
            group_scores = jnp.sum(jax.lax.top_k(swb.reshape(swb.shape[:-1] + (N_GROUP, -1)), 2)[0], axis=-1)
            group_idx = jax.lax.top_k(group_scores, TOPK_GROUP)[1]
            mask = jnp.any(jnp.arange(N_GROUP)[:, None] == group_idx[..., None, :], axis=-1)
            mask = jnp.repeat(mask, e // N_GROUP, axis=-1)
            masked_scores = jnp.where(mask, swb, 0.0)
            topk_idx = jax.lax.top_k(masked_scores, TOPK)[1]
            topk_w = jnp.take_along_axis(scores, topk_idx, axis=-1).astype(jnp.float32)
            topk_w = ROUTED_SCALE * topk_w / (jnp.sum(topk_w, axis=-1)[..., None] + 1e-20)
            return (topk_w, topk_idx)

        def _moe_forward(x, w_router, b_router, we_gate, we_up, we_down, ws_gate, ws_up, ws_down):
            b, s, d = x.shape
            e = we_gate.shape[0]
            topk_w, topk_idx = _route(x, w_router, b_router)
            x_flat = x.reshape(-1, d)
            idx_flat = topk_idx.reshape(-1)
            sort = jnp.argsort(idx_flat)
            tok = sort // TOPK
            x_sorted = x_flat[tok]
            group_sizes = jnp.bincount(idx_flat, length=e).astype(jnp.int32)
            g = jax.lax.ragged_dot(x_sorted, we_gate, group_sizes)
            u = jax.lax.ragged_dot(x_sorted, we_up, group_sizes)
            o = jax.lax.ragged_dot(jax.nn.silu(g) * u, we_down, group_sizes)
            w_sorted = topk_w.reshape(-1)[sort].astype(o.dtype)
            y = jnp.zeros_like(x_flat).at[tok].add(o * w_sorted[:, None])
            y = y.reshape(b, s, d)
            shared = jnp.einsum('btf,fd->btd', jax.nn.silu(jnp.einsum('btd,df->btf', x, ws_gate)) * jnp.einsum('btd,df->btf', x, ws_up), ws_down)
            return y + shared
        key = jax.random.key(seed)
        ks = jax.random.split(key, 10)
        sd = 1.0 / np.sqrt(D)
        sf = 1.0 / np.sqrt(F)
        return {'x': jax.random.normal(ks[0], (B, S, D), jnp.float32), 'w_router': jax.random.normal(ks[1], (D, E), jnp.float32) * sd, 'b_router': jax.random.normal(ks[2], (E,), jnp.float32) * 0.1, 'we_gate': jax.random.normal(ks[3], (E, D, F), jnp.float32) * sd, 'we_up': jax.random.normal(ks[4], (E, D, F), jnp.float32) * sd, 'we_down': jax.random.normal(ks[5], (E, F, D), jnp.float32) * sf, 'ws_gate': jax.random.normal(ks[6], (D, F), jnp.float32) * sd, 'ws_up': jax.random.normal(ks[7], (D, F), jnp.float32) * sd, 'ws_down': jax.random.normal(ks[8], (F, D), jnp.float32) * sf}
    _L0_ffn_all = _L0_ffn_setup()
    _L0_ffn_in = {k: v for k, v in _L0_ffn_all.items() if k in ('w_router', 'b_router', 'we_gate', 'we_up', 'we_down', 'ws_gate', 'ws_up', 'ws_down')}
    del _L0_ffn_all

    def _L1_attn_setup():
        import jax, jax.numpy as jnp
        import numpy as np
        import math
        B, T, D, H = (4, 512, 256, 16)
        HD = D // H
        ROPE_BASE = 10000.0

        def apply_rope(x):
            t, hd = (x.shape[2], x.shape[3])
            half = hd // 2
            theta = 1.0 / ROPE_BASE ** (jnp.arange(0, hd, 2, dtype=jnp.float32) / hd)
            pos = jnp.arange(1, t + 1, dtype=jnp.float32)
            ang = pos[:, None] * theta[None, :]
            ang = jnp.concatenate([ang, ang], axis=-1)
            sin, cos = (jnp.sin(ang), jnp.cos(ang))
            rot = jnp.concatenate([-x[..., half:], x[..., :half]], axis=-1)
            return x * cos[None, None, :, :] + rot * sin[None, None, :, :]
        key = jax.random.key(seed)
        ks = jax.random.split(key, 9)
        s = 1.0 / math.sqrt(D)
        return {'x': jax.random.normal(ks[0], (B, T, D), dtype=jnp.float32), 'Wq': jax.random.normal(ks[1], (D, D), dtype=jnp.float32) * s, 'bq': jax.random.normal(ks[2], (D,), dtype=jnp.float32) * 0.01, 'Wk': jax.random.normal(ks[3], (D, D), dtype=jnp.float32) * s, 'bk': jax.random.normal(ks[4], (D,), dtype=jnp.float32) * 0.01, 'Wv': jax.random.normal(ks[5], (D, D), dtype=jnp.float32) * s, 'bv': jax.random.normal(ks[6], (D,), dtype=jnp.float32) * 0.01, 'Wo': jax.random.normal(ks[7], (D, D), dtype=jnp.float32) * s, 'bo': jax.random.normal(ks[8], (D,), dtype=jnp.float32) * 0.01}
    _L1_attn_all = _L1_attn_setup()
    _L1_attn_in = {k: v for k, v in _L1_attn_all.items() if k in ('Wq', 'bq', 'Wk', 'bk', 'Wv', 'bv', 'Wo', 'bo')}
    del _L1_attn_all

    def _L1_xattn_setup():
        import jax, jax.numpy as jnp
        import numpy as np
        D_MODEL, D_K, D_V, H = (256, 64, 64, 16)
        B, NQ, NK, M = (8, 256, 256, 49)

        def _xavier(key, shape):
            fan_in, fan_out = (shape[1], shape[0])
            limit = float(np.sqrt(6.0 / (fan_in + fan_out)))
            return jax.random.uniform(key, shape, jnp.float32, -limit, limit)
        key = jax.random.key(seed)
        ks = jax.random.split(key, 12)
        inp = {'queries': jax.random.normal(ks[0], (B, NQ, D_MODEL), jnp.float32), 'keys': jax.random.normal(ks[1], (B, NK, D_MODEL), jnp.float32), 'values': jax.random.normal(ks[2], (B, NK, D_MODEL), jnp.float32), 'attention_mask': jax.random.randint(ks[3], (B, H, NQ, NK), 0, 2) > 0, 'key_grid': jax.random.normal(ks[4], (B, M, D_MODEL), jnp.float32), 'value_grid': jax.random.normal(ks[5], (B, M, D_MODEL), jnp.float32), 'Wq': _xavier(ks[6], (H * D_K, D_MODEL)), 'bq': jnp.zeros((H * D_K,), jnp.float32), 'Wk': _xavier(ks[7], (H * D_K, D_MODEL)), 'bk': jnp.zeros((H * D_K,), jnp.float32), 'Wgk': _xavier(ks[8], (H * D_K, D_MODEL)), 'bgk': jnp.zeros((H * D_K,), jnp.float32), 'Wv': _xavier(ks[9], (H * D_V, D_MODEL)), 'bv': jnp.zeros((H * D_V,), jnp.float32), 'Wgv': _xavier(ks[10], (H * D_V, D_MODEL)), 'bgv': jnp.zeros((H * D_V,), jnp.float32), 'Wo': _xavier(ks[11], (D_MODEL, H * D_V)), 'bo': jnp.zeros((D_MODEL,), jnp.float32)}
        return inp
    _L1_xattn_all = _L1_xattn_setup()
    _L1_xattn_in = {k: v for k, v in _L1_xattn_all.items() if k in ('Wq', 'bq', 'Wk', 'bk', 'Wgk', 'bgk', 'Wv', 'bv', 'Wgv', 'bgv', 'Wo', 'bo')}
    del _L1_xattn_all

    def _L1_ffn_setup():
        import jax, jax.numpy as jnp
        import numpy as np
        D_MODEL = 256
        NUM_EXPERTS = 8
        TOP_K = 2
        key = jax.random.key(seed)
        k_x, k_g, k_w1, k_w2 = jax.random.split(key, 4)
        B, S, D, E = (4, 512, D_MODEL, NUM_EXPERTS)
        s_in = 1.0 / np.sqrt(D)
        s_hid = 1.0 / np.sqrt(4 * D)
        return {'x': jax.random.normal(k_x, (B, S, D), dtype=jnp.float32), 'gate_w': jax.random.uniform(k_g, (E, D), jnp.float32, -s_in, s_in), 'w1': jax.random.uniform(k_w1, (E, 4 * D, D), jnp.float32, -s_in, s_in), 'w2': jax.random.uniform(k_w2, (E, D, 4 * D), jnp.float32, -s_hid, s_hid)}
    _L1_ffn_all = _L1_ffn_setup()
    _L1_ffn_in = {k: v for k, v in _L1_ffn_all.items() if k in ('gate_w', 'w1', 'w2')}
    del _L1_ffn_all
    return {'x': x, 'ctx_1024': ctx_1024, 'fside_BxSxS_0': fside_BxSxS_0, 'mask_Bx1x1xS2_ik0': mask_Bx1x1xS2_ik0, 'mask_Bx16xSxS_bk1': mask_Bx16xSxS_bk1, 'L0_attn_Wq': _L0_attn_in['Wq'], 'L0_attn_Wk': _L0_attn_in['Wk'], 'L0_attn_Wv': _L0_attn_in['Wv'], 'L0_attn_Wo': _L0_attn_in['Wo'], 'L0_xattn_Wq': _L0_xattn_in['Wq'], 'L0_xattn_bq': _L0_xattn_in['bq'], 'L0_xattn_Wk': _L0_xattn_in['Wk'], 'L0_xattn_bk': _L0_xattn_in['bk'], 'L0_xattn_Wv': _L0_xattn_in['Wv'], 'L0_xattn_bv': _L0_xattn_in['bv'], 'L0_xattn_Wo': _L0_xattn_in['Wo'], 'L0_xattn_bo': _L0_xattn_in['bo'], 'L0_ffn_w_router': _L0_ffn_in['w_router'], 'L0_ffn_b_router': _L0_ffn_in['b_router'], 'L0_ffn_we_gate': _L0_ffn_in['we_gate'], 'L0_ffn_we_up': _L0_ffn_in['we_up'], 'L0_ffn_we_down': _L0_ffn_in['we_down'], 'L0_ffn_ws_gate': _L0_ffn_in['ws_gate'], 'L0_ffn_ws_up': _L0_ffn_in['ws_up'], 'L0_ffn_ws_down': _L0_ffn_in['ws_down'], 'L1_attn_Wq': _L1_attn_in['Wq'], 'L1_attn_bq': _L1_attn_in['bq'], 'L1_attn_Wk': _L1_attn_in['Wk'], 'L1_attn_bk': _L1_attn_in['bk'], 'L1_attn_Wv': _L1_attn_in['Wv'], 'L1_attn_bv': _L1_attn_in['bv'], 'L1_attn_Wo': _L1_attn_in['Wo'], 'L1_attn_bo': _L1_attn_in['bo'], 'L1_xattn_Wq': _L1_xattn_in['Wq'], 'L1_xattn_bq': _L1_xattn_in['bq'], 'L1_xattn_Wk': _L1_xattn_in['Wk'], 'L1_xattn_bk': _L1_xattn_in['bk'], 'L1_xattn_Wgk': _L1_xattn_in['Wgk'], 'L1_xattn_bgk': _L1_xattn_in['bgk'], 'L1_xattn_Wv': _L1_xattn_in['Wv'], 'L1_xattn_bv': _L1_xattn_in['bv'], 'L1_xattn_Wgv': _L1_xattn_in['Wgv'], 'L1_xattn_bgv': _L1_xattn_in['bgv'], 'L1_xattn_Wo': _L1_xattn_in['Wo'], 'L1_xattn_bo': _L1_xattn_in['bo'], 'L1_ffn_gate_w': _L1_ffn_in['gate_w'], 'L1_ffn_w1': _L1_ffn_in['w1'], 'L1_ffn_w2': _L1_ffn_in['w2']}

def reference(x, ctx_1024, fside_BxSxS_0, mask_Bx1x1xS2_ik0, mask_Bx16xSxS_bk1, L0_attn_Wq, L0_attn_Wk, L0_attn_Wv, L0_attn_Wo, L0_xattn_Wq, L0_xattn_bq, L0_xattn_Wk, L0_xattn_bk, L0_xattn_Wv, L0_xattn_bv, L0_xattn_Wo, L0_xattn_bo, L0_ffn_w_router, L0_ffn_b_router, L0_ffn_we_gate, L0_ffn_we_up, L0_ffn_we_down, L0_ffn_ws_gate, L0_ffn_ws_up, L0_ffn_ws_down, L1_attn_Wq, L1_attn_bq, L1_attn_Wk, L1_attn_bk, L1_attn_Wv, L1_attn_bv, L1_attn_Wo, L1_attn_bo, L1_xattn_Wq, L1_xattn_bq, L1_xattn_Wk, L1_xattn_bk, L1_xattn_Wgk, L1_xattn_bgk, L1_xattn_Wv, L1_xattn_bv, L1_xattn_Wgv, L1_xattn_bgv, L1_xattn_Wo, L1_xattn_bo, L1_ffn_gate_w, L1_ffn_w1, L1_ffn_w2):
    import jax
    import jax.numpy as jnp

    def _L0_attn_ref(x, Wq, Wk, Wv, Wo):
        import jax, jax.numpy as jnp
        import numpy as np
        D_MODEL = 256
        N_HEADS = 16
        HEAD_DIM = D_MODEL // N_HEADS
        CHUNK = 128
        B, T = (2, 512)

        def _chunked_causal_attention(q, k, v, cs):
            Bq, H, Tq, D = q.shape
            n = Tq // cs
            inv_sqrt_d = 1.0 / D ** 0.5
            qc = jnp.moveaxis(q.reshape(Bq, H, n, cs, D), 2, 0)
            kc = jnp.moveaxis(k.reshape(Bq, H, n, cs, D), 2, 0)
            vc = jnp.moveaxis(v.reshape(Bq, H, n, cs, D), 2, 0)
            ar = jnp.arange(cs)

            def per_q(qi, qb):
                q_idx = qi * cs + ar

                def step(carry, kv):
                    m, l, o = carry
                    ki, kb, vb = kv
                    s = jnp.einsum('bhqd,bhkd->bhqk', qb, kb) * inv_sqrt_d
                    k_idx = ki * cs + ar
                    causal = q_idx[:, None] >= k_idx[None, :]
                    s = jnp.where(causal, s, -jnp.inf)
                    s_max = jnp.max(s, axis=-1, keepdims=True)
                    m_new = jnp.maximum(m, s_max)
                    m_safe = jnp.where(jnp.isneginf(m_new), 0.0, m_new)
                    alpha = jnp.exp(m - m_safe)
                    p = jnp.exp(s - m_safe)
                    o = o * alpha + jnp.einsum('bhqk,bhkd->bhqd', p, vb)
                    l = l * alpha + jnp.sum(p, axis=-1, keepdims=True)
                    return ((m_new, l, o), None)
                init = (jnp.full((Bq, H, cs, 1), -jnp.inf, dtype=jnp.float32), jnp.zeros((Bq, H, cs, 1), dtype=jnp.float32), jnp.zeros_like(qb))
                (m, l, o), _ = jax.lax.scan(step, init, (jnp.arange(n), kc, vc))
                return o / jnp.maximum(l, 1e-09)
            out = jax.vmap(per_q)(jnp.arange(n), qc)
            return jnp.moveaxis(out, 0, 2).reshape(Bq, H, Tq, D)
        Bx, Tx, C = x.shape

        def heads(w):
            return (x @ w.T).reshape(Bx, Tx, N_HEADS, HEAD_DIM).transpose(0, 2, 1, 3)
        q, k, v = (heads(Wq), heads(Wk), heads(Wv))
        y = _chunked_causal_attention(q, k, v, CHUNK)
        y = y.transpose(0, 2, 1, 3).reshape(Bx, Tx, C)
        return y @ Wo.T

    def _L0_xattn_ref(query, key, value, mask, Wq, bq, Wk, bk, Wv, bv, Wo, bo):
        import jax, jax.numpy as jnp
        import numpy as np
        D_MODEL = 256
        N_HEADS = 16
        HEAD_DIM = D_MODEL // N_HEADS
        B, S = (4, 512)
        NEG = -1000000000.0

        def _split_heads(x):
            b, s, _ = x.shape
            return x.reshape(b, s, N_HEADS, HEAD_DIM).transpose(0, 2, 1, 3)
        Q = _split_heads(query @ Wq.T + bq)
        K = _split_heads(key @ Wk.T + bk)
        V = _split_heads(value @ Wv.T + bv)
        scores = jnp.einsum('bhqd,bhkd->bhqk', Q, K) / np.sqrt(HEAD_DIM)
        scores = jnp.where(mask == 0, NEG, scores)
        probs = jax.nn.softmax(scores, axis=-1)
        ctx = jnp.einsum('bhqk,bhkd->bhqd', probs, V)
        ctx = ctx.transpose(0, 2, 1, 3).reshape(query.shape[0], query.shape[1], D_MODEL)
        return ctx @ Wo.T + bo

    def _L0_ffn_ref(x, w_router, b_router, we_gate, we_up, we_down, ws_gate, ws_up, ws_down):
        import jax, jax.numpy as jnp
        import numpy as np
        N_GROUP = 8
        TOPK_GROUP = 4
        TOPK = 8
        ROUTED_SCALE = 2.5
        B, S, D, F, E = (4, 512, 256, 128, 64)

        def _route(x, w_router, b_router):
            scores = jax.nn.sigmoid(jnp.einsum('bsd,de->bse', x, w_router)).astype(jnp.float32)
            swb = scores + b_router
            e = scores.shape[-1]
            group_scores = jnp.sum(jax.lax.top_k(swb.reshape(swb.shape[:-1] + (N_GROUP, -1)), 2)[0], axis=-1)
            group_idx = jax.lax.top_k(group_scores, TOPK_GROUP)[1]
            mask = jnp.any(jnp.arange(N_GROUP)[:, None] == group_idx[..., None, :], axis=-1)
            mask = jnp.repeat(mask, e // N_GROUP, axis=-1)
            masked_scores = jnp.where(mask, swb, 0.0)
            topk_idx = jax.lax.top_k(masked_scores, TOPK)[1]
            topk_w = jnp.take_along_axis(scores, topk_idx, axis=-1).astype(jnp.float32)
            topk_w = ROUTED_SCALE * topk_w / (jnp.sum(topk_w, axis=-1)[..., None] + 1e-20)
            return (topk_w, topk_idx)

        def _moe_forward(x, w_router, b_router, we_gate, we_up, we_down, ws_gate, ws_up, ws_down):
            b, s, d = x.shape
            e = we_gate.shape[0]
            topk_w, topk_idx = _route(x, w_router, b_router)
            x_flat = x.reshape(-1, d)
            idx_flat = topk_idx.reshape(-1)
            sort = jnp.argsort(idx_flat)
            tok = sort // TOPK
            x_sorted = x_flat[tok]
            group_sizes = jnp.bincount(idx_flat, length=e).astype(jnp.int32)
            g = jax.lax.ragged_dot(x_sorted, we_gate, group_sizes)
            u = jax.lax.ragged_dot(x_sorted, we_up, group_sizes)
            o = jax.lax.ragged_dot(jax.nn.silu(g) * u, we_down, group_sizes)
            w_sorted = topk_w.reshape(-1)[sort].astype(o.dtype)
            y = jnp.zeros_like(x_flat).at[tok].add(o * w_sorted[:, None])
            y = y.reshape(b, s, d)
            shared = jnp.einsum('btf,fd->btd', jax.nn.silu(jnp.einsum('btd,df->btf', x, ws_gate)) * jnp.einsum('btd,df->btf', x, ws_up), ws_down)
            return y + shared
        return _moe_forward(x, w_router, b_router, we_gate, we_up, we_down, ws_gate, ws_up, ws_down)

    def _L1_attn_ref(x, Wq, bq, Wk, bk, Wv, bv, Wo, bo):
        import jax, jax.numpy as jnp
        import numpy as np
        import math
        B, T, D, H = (4, 512, 256, 16)
        HD = D // H
        ROPE_BASE = 10000.0

        def apply_rope(x):
            t, hd = (x.shape[2], x.shape[3])
            half = hd // 2
            theta = 1.0 / ROPE_BASE ** (jnp.arange(0, hd, 2, dtype=jnp.float32) / hd)
            pos = jnp.arange(1, t + 1, dtype=jnp.float32)
            ang = pos[:, None] * theta[None, :]
            ang = jnp.concatenate([ang, ang], axis=-1)
            sin, cos = (jnp.sin(ang), jnp.cos(ang))
            rot = jnp.concatenate([-x[..., half:], x[..., :half]], axis=-1)
            return x * cos[None, None, :, :] + rot * sin[None, None, :, :]
        b, t, d = x.shape
        h, hd = (H, HD)
        q = x @ Wq.T + bq
        k = x @ Wk.T + bk
        v = x @ Wv.T + bv
        split = lambda z: z.reshape(b, t, h, hd).transpose(0, 2, 1, 3)
        q, k, v = (split(q), split(k), split(v))
        q = apply_rope(q)
        k = apply_rope(k)
        scale = math.sqrt(hd)
        att = jnp.einsum('bhqd,bhkd->bhqk', q, k) / scale
        mask = jnp.tril(jnp.ones((t, t), dtype=bool))
        att = jnp.where(mask[None, None, :, :], att, -jnp.inf)
        att = jax.nn.softmax(att, axis=-1)
        y = jnp.einsum('bhqk,bhkd->bhqd', att, v)
        y = y.transpose(0, 2, 1, 3).reshape(b, t, d)
        y = y @ Wo.T + bo
        return y

    def _L1_xattn_ref(queries, keys, values, attention_mask, key_grid, value_grid, Wq, bq, Wk, bk, Wgk, bgk, Wv, bv, Wgv, bgv, Wo, bo):
        import jax, jax.numpy as jnp
        import numpy as np
        D_MODEL, D_K, D_V, H = (256, 64, 64, 16)
        B, NQ, NK, M = (8, 256, 256, 49)

        def _xavier(key, shape):
            fan_in, fan_out = (shape[1], shape[0])
            limit = float(np.sqrt(6.0 / (fan_in + fan_out)))
            return jax.random.uniform(key, shape, jnp.float32, -limit, limit)
        b_s, nq, _ = queries.shape
        nk = keys.shape[1]
        scale = 1.0 / np.sqrt(D_K)
        k = keys @ Wk.T + bk
        gk = key_grid @ Wgk.T + bgk
        k_new = jnp.concatenate([k, gk], axis=1)
        k_new = k_new.reshape(b_s, -1, H, D_K).transpose(0, 2, 3, 1)
        v = values @ Wv.T + bv
        gv = key_grid @ Wgv.T + bgv
        v_new = jnp.concatenate([v, gv], axis=1)
        v_new = v_new.reshape(b_s, -1, H, D_V).transpose(0, 2, 1, 3)
        q = (queries @ Wq.T + bq).reshape(b_s, nq, H, D_K).transpose(0, 2, 1, 3)
        att = jnp.einsum('bhqd,bhdk->bhqk', q, k_new) * scale
        att_k = jnp.where(attention_mask, -jnp.inf, att[..., :nk])
        att = jnp.concatenate([att_k, att[..., nk:]], axis=-1)
        att = jax.nn.softmax(att, axis=-1)
        out = jnp.einsum('bhqk,bhkd->bhqd', att, v_new)
        out = out.transpose(0, 2, 1, 3).reshape(b_s, nq, H * D_V)
        return out @ Wo.T + bo

    def _L1_ffn_ref(x, gate_w, w1, w2):
        import jax, jax.numpy as jnp
        import numpy as np
        D_MODEL = 256
        NUM_EXPERTS = 8
        TOP_K = 2
        gate_logits = jnp.einsum('bsd,ed->bse', x, gate_w)
        top_v, top_i = jax.lax.top_k(gate_logits, TOP_K)
        gates = jax.nn.softmax(top_v, axis=-1)
        combine = jnp.sum(jax.nn.one_hot(top_i, NUM_EXPERTS, dtype=x.dtype) * gates[..., None], axis=-2)
        out = jnp.zeros_like(x)
        for e in range(NUM_EXPERTS):
            h = jax.nn.relu(jnp.einsum('bsd,fd->bsf', x, w1[e]))
            y = jnp.einsum('bsf,df->bsd', h, w2[e])
            out = out + combine[..., e, None] * y
        return out
    x = x + _L0_attn_ref(_layernorm(x, axis=-1), L0_attn_Wq, L0_attn_Wk, L0_attn_Wv, L0_attn_Wo)
    x = x + _L0_xattn_ref(_layernorm(x, axis=-1), ctx_1024, ctx_1024, mask_Bx1x1xS2_ik0, L0_xattn_Wq, L0_xattn_bq, L0_xattn_Wk, L0_xattn_bk, L0_xattn_Wv, L0_xattn_bv, L0_xattn_Wo, L0_xattn_bo)
    x = x + _L0_ffn_ref(_layernorm(x, axis=-1), L0_ffn_w_router, L0_ffn_b_router, L0_ffn_we_gate, L0_ffn_we_up, L0_ffn_we_down, L0_ffn_ws_gate, L0_ffn_ws_up, L0_ffn_ws_down)
    x = x + _L1_attn_ref(_layernorm(x, axis=-1), L1_attn_Wq, L1_attn_bq, L1_attn_Wk, L1_attn_bk, L1_attn_Wv, L1_attn_bv, L1_attn_Wo, L1_attn_bo)
    x = x + _L1_xattn_ref(_layernorm(x, axis=-1), fside_BxSxS_0, fside_BxSxS_0, mask_Bx16xSxS_bk1, ctx_1024, ctx_1024, L1_xattn_Wq, L1_xattn_bq, L1_xattn_Wk, L1_xattn_bk, L1_xattn_Wgk, L1_xattn_bgk, L1_xattn_Wv, L1_xattn_bv, L1_xattn_Wgv, L1_xattn_bgv, L1_xattn_Wo, L1_xattn_bo)
    x = x + _L1_ffn_ref(_layernorm(x, axis=-1), L1_ffn_gate_w, L1_ffn_w1, L1_ffn_w2)
    return x

_drawn_inputs = setup_inputs


def setup_inputs(seed=0):
    import zlib

    import numpy as np

    out = dict(_drawn_inputs(seed))
    spreads = {'L1_xattn_bq': (0.0, 0.8),
     'L1_xattn_bk': (0.0, 2.0),
     'L1_xattn_bgk': (0.0, 2.0),
     'L1_xattn_bv': (0.0, 0.645),
     'L1_xattn_bgv': (0.0, 2.0),
     'L1_xattn_bo': (0.0, 0.8)}
    factors = {'fside_BxSxS_0': 3.894,
     'L0_attn_Wq': 3.571,
     'L0_attn_Wk': 3.396,
     'L0_xattn_bk': 200.0,
     'L1_attn_bq': 25.783,
     'L1_attn_bk': 37.798,
     'L1_attn_bv': 5.523,
     'L1_attn_bo': 6.183,
     'L1_xattn_Wk': 7.237,
     'L1_xattn_Wv': 4.009,
     'L1_xattn_Wgk': 8.0,
     'L1_xattn_Wgv': 8.0,
     'L1_ffn_gate_w': 4.566,
     'L1_ffn_w1': 4.836,
     'L1_ffn_w2': 3.984}
    for name, (base, spread) in spreads.items():
        noise = np.random.default_rng([zlib.crc32(name.encode()), seed]).standard_normal(out[name].shape)
        drawn = base * np.exp(spread * noise) if base else spread * noise
        out[name] = jnp.asarray(drawn.astype(out[name].dtype))
    for name, factor in factors.items():
        out[name] = (out[name] * factor).astype(out[name].dtype)
    return out
```

```python
from contextlib import ExitStack

import concourse.bass as bass
from concourse import mybir

F32 = mybir.dt.float32
BF16 = mybir.dt.bfloat16
I32 = mybir.dt.int32
ACT = mybir.ActivationFunctionType
ALU = mybir.AluOpType
AX = mybir.AxisListType

P = 128
B, S, D = 16, 256, 256
H = 16
TT = S // P
DC = D // P
TILES = B * TT
LN_EPS = 1e-5
MASKED = -1e9
LOW = -1e30
STAGES = 6

class Attn:

    def __init__(self, name, dk, keys, causal=False, rope=False, keymask=False, fullmask=False):
        self.name, self.dk, self.keys = name, dk, keys
        self.causal, self.rope, self.keymask, self.fullmask = causal, rope, keymask, fullmask
        self.cross = keymask or fullmask
        self.wide = fullmask
        self.hpc = 1024 // keys
        self.chunks = H // self.hpc
        self.steps = self.chunks * TT
        self.inner = H * dk
        self.groups = self.inner // P
        self.kt = keys // P
        self.m = P // self.hpc
        self.scale = dk ** -0.5

    def key_tiles(self, t):
        return t + 1 if self.causal else self.kt

ATTN = {
    "L0_attn": Attn("L0_attn", 16, S, causal=True),
    "L0_xattn": Attn("L0_xattn", 16, S, keymask=True),
    "L1_attn": Attn("L1_attn", 16, S, causal=True, rope=True),
    "L1_xattn": Attn("L1_xattn", 64, 2 * S, fullmask=True),
}

def tile_pair(x_res, b):
    return x_res[:, bass.ds(b * TT, TT), :]

def attention_phase(nc, c, x_res, ident, ins):
    n = c.name
    with ExitStack() as ctx:
        def sb(name, shape, dt=F32):
            return ctx.enter_context(nc.sbuf_tensor(f"{n}_{name}", shape, dt))

        def sem(name):
            return nc.alloc_semaphore(name=f"{n}_{name}")

        ps = [ctx.enter_context(nc.psum_tensor(f"{n}_bank{i}", [P, 512], F32)) for i in range(4, 8)]
        s_ps = [ctx.enter_context(nc.psum_tensor(f"{n}_scores{i}", [P, c.hpc, c.keys], F32)) for i in range(2)]
        t_ps, a_ps = ps[0:2], ps[2:4]

        wq = sb("wq", [P, DC, c.inner])
        wk = sb("wk", [P, DC, c.inner])
        wv = sb("wv", [P, DC, c.inner])
        wo = sb("wo", [P, c.chunks, D])
        bq = sb("bq", [P, c.groups])
        bk = sb("bk", [P, c.groups])
        bv = sb("bv", [1, c.inner])
        bo = sb("bo", [1, D])
        ones = sb("ones", [1, P])
        loads = [(wq, "wq"), (wk, "wk"), (wv, "wv"), (wo, "wo"), (bq, "bq"), (bk, "bk"), (bv, "bv"), (bo, "bo")]
        if c.rope:
            wqr = sb("wqr", [P, DC, D])
            wkr = sb("wkr", [P, DC, D])
            bqr = sb("bqr", [P, c.groups])
            bkr = sb("bkr", [P, c.groups])
            cos = sb("cos", [P, S])
            sin = sb("sin", [P, S])
            loads += [(wqr, "wqr"), (wkr, "wkr"), (bqr, "bqr"), (bkr, "bkr"), (cos, "cos"), (sin, "sin")]
        if c.wide:
            wgk = sb("wgk", [P, DC, c.inner])
            wgv = sb("wgv", [P, DC, c.inner])
            bgk = sb("bgk", [P, c.groups])
            bgv = sb("bgv", [1, c.inner])
            loads += [(wgk, "wgk"), (wgv, "wgv"), (bgk, "bgk"), (bgv, "bgv")]
            low_ident = sb("low_ident", [P, P], BF16)
            loads += [(low_ident, "low_ident")]
        else:
            headmask = sb("headmask", [P, 8])
            loads += [(headmask, "headmask")]
        if c.causal:
            ident_bf = sb("ident_bf", [P, P], BF16)
            tri = sb("tri", [P, P], BF16)
            loads += [(ident_bf, "ident_bf"), (tri, "tri")]
        if c.keymask:
            masked3 = sb("masked3", [3, P], BF16)
            loads += [(masked3, "masked3")]

        stats = sb("stats", [P, TT, 6])
        mv = sb("mv", [P, TT, 2])
        rstd = sb("rstd", [P, TT])
        eps_t = sb("eps", [P, TT])
        power = sb("power", [P, TT])
        z = sb("z", [P, TT, D])
        zT = sb("zT", [P, DC, S])
        if c.cross:
            src = sb("src", [P, TT, D])
            srcT = sb("srcT", [P, DC, S])
        else:
            srcT = zT
        if c.wide:
            grid = sb("grid", [P, TT, D])
            gridT = sb("gridT", [P, DC, S])
            qT = sb("qT", [P, H, S])
            kT = sb("kT", [P, c.groups, c.keys])
            v = sb("v", [P, c.kt, H, c.dk])
            mask = sb("mask", [P, 4, c.hpc, S], BF16)
        else:
            qT = sb("qT", [P, c.groups, S])
            kT1 = sb("kT1", [P, c.groups, S])
            kT = sb("kT", [P, H, S])
            v = sb("v", [P, c.kt, H, c.m])
        if c.rope:
            qr = sb("qr", [P, c.groups, S])
            q0 = sb("q0", [P, c.groups, S])
            kr = sb("kr", [P, c.groups, S])
        if c.keymask:
            mask_i = sb("mask_i", [P, S], I32)
            keep = sb("keep", [P, S])
            drop3 = sb("drop3", [3, S], BF16)
        negmax = sb("negmax", [P, 2, c.hpc])
        lsum = sb("lsum", [P, 2, c.hpc])
        rsum = sb("rsum", [P, 2, c.hpc])
        p = sb("p", [P, 2, c.hpc, c.keys])
        pT = sb("pT", [P, 2, 8, S])
        yT = sb("yT", [P, c.chunks, S])

        loaded = sem("loaded")
        gp_set = sem("gp_set")
        in_loaded = sem("in_loaded")
        in_used = sem("in_used")
        z_ready = sem("z_ready")
        var_ready = sem("var_ready")
        rstd_ready = sem("rstd_ready")
        a_ready = [sem(f"a_ready{i}") for i in range(2)]
        a_free = [sem(f"a_free{i}") for i in range(2)]
        kv_ready = sem("kv_ready")
        src_k = sem("src_k")
        src_q = sem("src_q")
        s_ready = sem("s_ready")
        m_ready = sem("m_ready")
        p_ready = sem("p_ready")
        r_ready = sem("r_ready")
        n_ready = sem("n_ready")
        t_ready = sem("t_ready")
        t_done = sem("t_done")
        mask_in = [sem(f"mask_in{i}") for i in range(4)]
        keep_ready = sem("keep_ready")

        NS, NCH = c.steps, c.chunks

        uses = ["zT"]
        if c.cross:
            uses.append("srcT")
        if c.wide:
            uses.append("gridT")
        gpu = 2
        uses += [f"q{i}" for i in range(c.groups // gpu)]
        if c.rope:
            uses += ["qr"]
        if c.wide:
            uses += [f"k{i}" for i in range(c.groups)]
            uses += [f"v{i}" for i in range(2 * c.kt)]
        else:
            uses += ["k"] + (["kr"] if c.rope else []) + ["v"]
        if (len(uses) + NCH + 1) % 2:
            uses.append("pad")
        prologue = list(uses)
        uses += [f"o{i}" for i in range(NCH)] + ["out"]
        UA = len(uses) // 2
        at = {u: i for i, u in enumerate(uses)}

        def bank_wait_free(pe, b, use):
            i = at[use]
            pe.wait_ge(a_free[i % 2], b * UA + i // 2 + 1)
            return a_ps[i % 2], a_ready[i % 2]

        def bank_wait_ready(eng, b, use):
            i = at[use]
            eng.wait_ge(a_ready[i % 2], b * UA + i // 2 + 1)
            return a_ps[i % 2], a_free[i % 2]

        with nc.Block() as block:

            @block.sync
            def _(sp):
                for dst, key in loads:
                    sp.dma_start(dst[:], ins[key]).then_inc(loaded, 16)
                if c.cross:
                    with sp.Fori(0, B, 1) as b:
                        sp.wait_ge(in_used, b * 1 + 1)
                        sp.dma_start(src[:, :, :], ins["src"][bass.ds(b, 1), :, :].rearrange("b (t p) d -> p (b t) d", p=P)).then_inc(in_loaded, 16)
                        if c.wide:
                            sp.dma_start(grid[:, :, :], ins["grid"][bass.ds(b, 1), :, :].rearrange("b (t p) d -> p (b t) d", p=P)).then_inc(in_loaded, 16)
                        if c.keymask:
                            sp.dma_start(mask_i[:, :], ins["mask"][bass.ds(b, 1), :].partition_broadcast(P).rearrange("p b k -> p (b k)")).then_inc(in_loaded, 16)

            @block.gpsimd
            def _(pool):
                pool.memset(eps_t[:, :], LN_EPS).then_inc(gp_set, 1)
                pool.memset(power[:, :], -0.5).then_inc(gp_set, 1)
                if c.wide:
                    pool.memset(qT[:, :, :], 0.0).then_inc(gp_set, 1)
                else:
                    pool.memset(v[:, :, :, :], 0.0).then_inc(gp_set, 1)
                pool.memset(ones[:, :], 1.0).then_inc(gp_set, 1)
                pool.wait_ge(gp_set, 4)
                pool.wait_ge(loaded, 16 * len(loads))
                with pool.Fori(0, B, 1) as b:
                    if c.wide:
                        def load_mask(s):
                            ch, t = s // TT, s % TT
                            pool.dma_start(mask[:, s % 4, :, :], ins["mask"][bass.ds(b, 1), ch * c.hpc:(ch + 1) * c.hpc, t * P:(t + 1) * P, :].rearrange("b h p k -> p (b h) k")).then_inc(mask_in[s % 4], 16)
                        pool.wait_ge(s_ready, b * NS + 1)
                        for s in range(4):
                            load_mask(s)
                    pool.wait_ge(var_ready, b + 1)
                    pool.tensor_tensor(mv[:, :, 1], mv[:, :, 1], eps_t[:, :], ALU.add)
                    pool.drain()
                    pool.tensor_tensor(rstd[:, :], mv[:, :, 1], power[:, :], ALU.pow).then_inc(rstd_ready, 1)
                    if not c.wide:
                        if c.rope:
                            for i, (a, r) in enumerate(((q0, qr), (kT1, kr))):
                                pool.wait_ge(src_k if i else src_q, b * 2 + 2)
                                pool.tensor_tensor(a[:, :, :], a[:, :, :], cos[:, None, :].to_broadcast([P, c.groups, S]), ALU.mult)
                                pool.tensor_tensor(r[:, :, :], r[:, :, :], sin[:, None, :].to_broadcast([P, c.groups, S]), ALU.mult)
                                pool.drain()
                                pool.tensor_tensor(qT[:, :, :] if i == 0 else a[:, :, :], a[:, :, :], r[:, :, :], ALU.add)
                            pool.drain()
                        else:
                            pool.wait_ge(src_k, b + 1)
                        for g in range(c.groups):
                            e = pool.tensor_tensor(kT[:, 8 * g:8 * g + 8, :], kT1[:, g:g + 1, :].to_broadcast([P, 8, S]),
                                                   headmask[:, :, None].to_broadcast([P, 8, S]), ALU.mult)
                        e.then_inc(kv_ready, 1)
                    for s in range(NS):
                        t = s % TT
                        nk = P * c.key_tiles(t)
                        if c.wide and s >= 1 and s + 3 < NS:
                            pool.wait_ge(s_ready, b * NS + s + 1)
                            load_mask(s + 3)
                        pool.wait_ge(r_ready, b * NS + s + 1)
                        pool.tensor_tensor(p[:, s % 2, :, 0:nk], p[:, s % 2, :, 0:nk],
                                           rsum[:, s % 2, :, None].to_broadcast([P, c.hpc, nk]), ALU.mult).then_inc(n_ready, 1)

            @block.vector
            def _(dve):
                for k in range(2):
                    dve.sem_inc(a_free[k], 1)
                if c.wide:
                    dve.sem_inc(s_ready, 1)
                if c.cross:
                    dve.sem_inc(in_used, 1)
                dve.wait_ge(loaded, 16 * len(loads))
                dve.wait_ge(gp_set, 4)
                with dve.Fori(0, B, 1) as b:
                    for t in range(TT):
                        dve.bn_stats(stats[:, t, :], x_res[:, bass.ds(b * TT + t, 1), :])
                    dve.drain()
                    for t in range(TT):
                        e = dve.bn_aggr(mv[:, t, :], stats[:, t, :])
                    e.then_inc(var_ready, 1)
                    dve.drain()
                    dve.wait_ge(rstd_ready, b + 1)
                    for t in range(TT):
                        e = dve.tensor_scalar(z[:, t, :], x_res[:, bass.ds(b * TT + t, 1), :], mv[:, t, 0:1], rstd[:, t:t + 1], ALU.subtract, ALU.mult)
                    e.then_inc(z_ready, 1)
                    if c.keymask:
                        dve.wait_ge(in_loaded, b * 32 + 32)
                        dve.tensor_scalar(keep[:, :], mask_i[:, :], 0, None, ALU.not_equal)
                        dve.tensor_scalar(drop3[:, :], mask_i[0:3, :], 0, None, ALU.is_equal).then_inc(keep_ready, 1)
                    for i in range(c.groups // gpu):
                        bank, free = bank_wait_ready(dve, b, f"q{i}")
                        for j in range(gpu):
                            g = i * gpu + j
                            if c.wide:
                                for r in range(2):
                                    rows = slice(64 * r, 64 * r + 64)
                                    e = dve.tensor_scalar(qT[rows, 2 * g + r, :], bank[rows, j * S:(j + 1) * S], bq[rows, g:g + 1], c.scale, ALU.add, ALU.mult)
                            else:
                                e = dve.tensor_scalar((q0 if c.rope else qT)[:, g, :], bank[:, j * S:(j + 1) * S], bq[:, g:g + 1], c.scale, ALU.add, ALU.mult)
                        e.then_inc(free, 1)
                        if c.rope:
                            dve.drain().then_inc(src_q, 1)
                            bank, free = bank_wait_ready(dve, b, "qr")
                            for g in range(c.groups):
                                e = dve.tensor_scalar(qr[:, g, :], bank[:, g * S:(g + 1) * S], bqr[:, g:g + 1], c.scale, ALU.add, ALU.mult)
                            e.then_inc(free, 1)
                            dve.drain().then_inc(src_q, 1)
                    if c.keymask:
                        dve.drain()
                        bank, free = bank_wait_ready(dve, b, "k")
                        for g in range(c.groups):
                            e = dve.scalar_tensor_tensor(kT1[:, g, :], bank[:, g * S:(g + 1) * S], bk[:, g:g + 1], keep[:, :], ALU.add, ALU.mult)
                        e.then_inc(free, 1)
                        dve.drain().then_inc(src_k, 1)

                    def row_max(s):
                        t = s % TT
                        nk = P * c.key_tiles(t)
                        dve.wait_ge(s_ready, b * NS + s + 1 + int(c.wide))
                        dve.tensor_reduce(negmax[:, s % 2, :], s_ps[s % 2][:, :, 0:nk], AX.X, ALU.max, negate=True).then_inc(m_ready, 1)

                    row_max(0)
                    for s in range(NS):
                        ch, t = s // TT, s % TT
                        if s + 1 < NS:
                            row_max(s + 1)
                        dve.wait_ge(p_ready, b * NS + s + 1)
                        dve.reciprocal(rsum[:, s % 2, :], lsum[:, s % 2, :]).then_inc(r_ready, 1)
                        for hh in range(2):
                            dve.wait_ge(t_ready, (b * NS + s) * 2 + hh + 1)
                            dst = pT[:, ch % 2, 4 * hh:4 * hh + 4, t * P:(t + 1) * P]
                            view = t_ps[hh][:, :].rearrange("p (a q) -> p a q", q=P)
                            if c.key_tiles(t) == 1:
                                dst = pT[:, ch % 2, 4 * hh:4 * hh + 3:2, t * P:(t + 1) * P]
                                view = view[:, 0:3:2, :]
                            dve.tensor_copy(dst, view).then_inc(t_done, 1)
                    bank, free = bank_wait_ready(dve, b, "out")
                    dve.tensor_tensor(tile_pair(x_res, b), bank[:, :].rearrange("p (t d) -> p t d", d=D), tile_pair(x_res, b), ALU.add).then_inc(free, 1)

            @block.scalar
            def _(act):
                act.wait_ge(loaded, 16 * len(loads))
                act.wait_ge(gp_set, 4)
                with act.Fori(0, B, 1) as b:
                    def copy_out(use, pieces):
                        bank, free = bank_wait_ready(act, b, use)
                        for dst, src_ap, bias in pieces(bank):
                            if bias is None:
                                e = act.activation(dst, src_ap, ACT.Copy)
                            else:
                                e = act.activation(dst, src_ap, ACT.Identity, bias=bias)
                        e.then_inc(free, 1)
                        return e

                    def half(bank, j):
                        return bank[:, j * S:(j + 1) * S]

                    for u in prologue:
                        if u in ("zT", "srcT", "gridT"):
                            dst = {"zT": zT, "srcT": srcT}.get(u) if u != "gridT" else gridT
                            copy_out(u, lambda bank: [(dst[:, :, :], bank[:, :].rearrange("p (c q) -> p c q", q=S), None)])
                        elif u == "k" and not c.keymask:
                            copy_out(u, lambda bank: [(kT1[:, g, :], half(bank, g), bk[:, g:g + 1]) for g in range(c.groups)])
                            act.drain().then_inc(src_k, 1)
                        elif u == "kr":
                            copy_out(u, lambda bank: [(kr[:, g, :], half(bank, g), bkr[:, g:g + 1]) for g in range(c.groups)])
                            act.drain().then_inc(src_k, 1)
                        elif u == "v":
                            copy_out(u, lambda bank: [(v[:, :, :, 0:c.dk], bank[:, :].rearrange("p (t h d) -> p t h d", t=TT, d=c.dk), None)])
                        elif u == "pad":
                            copy_out(u, lambda bank: [(yT[0:1, 0, 0:1], bank[0:1, 0:1], None)])
                        elif c.wide and u[0] == "k":
                            g = int(u[1:])
                            copy_out(u, lambda bank: [(kT[:, g, 0:S], half(bank, 0), bk[:, g:g + 1]), (kT[:, g, S:2 * S], half(bank, 1), bgk[:, g:g + 1])])
                        elif c.wide and u[0] == "v":
                            i = int(u[1:])
                            copy_out(u, lambda bank: [(v[:, i // 2, 8 * (i % 2):8 * (i % 2) + 8, :], bank[:, :].rearrange("p (h d) -> p h d", d=c.dk), None)])
                    for s in range(NS):
                        t = s % TT
                        nk = P * c.key_tiles(t)
                        act.wait_ge(m_ready, b * NS + s + 1)
                        if s >= 2:
                            act.wait_ge(t_ready, (b * NS + s - 1) * 2)
                        for i in range(c.hpc):
                            e = act.activation(p[:, s % 2, i, 0:nk], s_ps[s % 2][:, i, 0:nk], ACT.Exp, bias=negmax[:, s % 2, i:i + 1], accum_out=lsum[:, s % 2, i:i + 1])
                        e.then_inc(p_ready, 1)
                        if s >= 2 and t == 0:
                            ch = s // TT - 1
                            copy_out(f"o{ch}", lambda bank: [(yT[:, ch, :], half(bank, 0), None)])
                    copy_out(f"o{NCH - 1}", lambda bank: [(yT[:, NCH - 1, :], half(bank, 0), None)])

            @block.tensor
            def _(pe):
                pe.wait_ge(loaded, 16 * len(loads))
                pe.wait_ge(gp_set, 4)
                with pe.Fori(0, B, 1) as b:
                    def transposes(use, tiles):
                        bank, ready = bank_wait_free(pe, b, use)
                        for cc in range(DC):
                            for t in range(TT):
                                e = pe.transpose(bank[:, cc * S + t * P:cc * S + (t + 1) * P], tiles[:, t, cc * P:(cc + 1) * P], ident[:, :])
                        e.then_inc(ready, 1)

                    def project(out, w, g, xT):
                        for cc in range(DC):
                            e = pe.matmul(out, w[:, cc, g * P:(g + 1) * P], xT[:, cc, :], start=cc == 0, stop=cc == DC - 1)
                        return e

                    def project_rows(out, xT, t, w, c0, cols, bias):
                        for cc in range(DC):
                            pe.matmul(out, xT[:, cc, t * P:(t + 1) * P], w[:, cc, c0:c0 + cols], start=cc == 0, stop=False)
                        return pe.matmul(out, ones[:, :], bias[:, c0:c0 + cols], start=False, stop=True)

                    for u in prologue:
                        if u == "zT":
                            pe.wait_ge(z_ready, b + 1)
                            transposes("zT", z)
                        elif u == "srcT":
                            per = 16 * (1 + int(c.wide) + int(c.keymask))
                            pe.wait_ge(in_loaded, b * per + per)
                            transposes("srcT", src)
                        elif u == "gridT":
                            transposes("gridT", grid)
                        elif u == "pad":
                            bank, ready = bank_wait_free(pe, b, u)
                            pe.matmul(bank[:, 0:P], ident[:, :], ident[:, :], start=True, stop=True).then_inc(ready, 1)
                        else:
                            if u == "q0":
                                for last in ("zT", "srcT", "gridT")[:1 + int(c.cross) + int(c.wide)]:
                                    pe.wait_ge(a_free[at[last] % 2], b * UA + at[last] // 2 + 2)
                            bank, ready = bank_wait_free(pe, b, u)
                            if u[0] == "q":
                                w = wqr if u == "qr" else wq
                                i = 0 if u == "qr" else int(u[1:])
                                for j in range(gpu):
                                    e = project(bank[:, j * S:(j + 1) * S], w, i * gpu + j, zT)
                            elif u in ("k", "kr"):
                                for g in range(c.groups):
                                    e = project(bank[:, g * S:(g + 1) * S], wk if u == "k" else wkr, g, srcT)
                            elif u == "v":
                                for t in range(TT):
                                    e = project_rows(bank[:, t * D:(t + 1) * D], srcT, t, wv, 0, D, bv)
                            elif u[0] == "k":
                                g = int(u[1:])
                                project(bank[:, 0:S], wk, g, srcT)
                                e = project(bank[:, S:2 * S], wgk, g, gridT)
                            else:
                                i = int(u[1:])
                                kt, cols = i // 2, 512
                                own = kt < TT
                                e = project_rows(bank[:, :], srcT if own else gridT, kt % TT, wv if own else wgv, (i % 2) * cols, cols, bv if own else bgv)
                            e.then_inc(ready, 1)
                    for u in prologue[-2:]:
                        pe.wait_ge(a_free[at[u] % 2], b * UA + at[u] // 2 + 2)
                    if not c.wide:
                        pe.wait_ge(kv_ready, b + 1)
                    if c.keymask:
                        pe.wait_ge(keep_ready, b + 1)

                    def scores(s):
                        ch, t = s // TT, s % TT
                        nk = P * c.key_tiles(t)
                        out = s_ps[s % 2]
                        q0_, q1_ = t * P, (t + 1) * P
                        if c.wide:
                            pe.wait_ge(mask_in[s % 4], (b * (NS // 4) + s // 4) * 16 + 16)
                            for i in range(c.hpc):
                                pe.matmul(out[:, i, :], qT[:, ch * c.hpc + i, q0_:q1_], kT[:, ch, :], start=True, stop=False, skip_group_check=True)
                                e = pe.matmul(out[:, i, 0:S], low_ident[:, :], mask[:, s % 4, i, :], start=False, stop=True, skip_group_check=True)
                        else:
                            g = ch // 2
                            for hh in range(2):
                                h0 = ch * 4 + hh * 2
                                o = out[:, 2 * hh:2 * hh + 2, 0:nk]
                                e = pe.matmul(o, qT[:, g, q0_:q1_], kT[:, h0:h0 + 2, 0:nk], start=True, stop=not (c.causal or c.keymask), skip_group_check=True)
                                if c.causal:
                                    e = pe.matmul(out[:, 2 * hh:2 * hh + 2, q0_:q1_], ident_bf[:, :], tri[:, None, :].to_broadcast([P, 2, P]), start=False, stop=True, skip_group_check=True)
                                if c.keymask:
                                    e = pe.matmul(o, masked3[:, :], drop3[:, None, :].to_broadcast([3, 2, S]), start=False, stop=True, skip_group_check=True)
                        e.then_inc(s_ready, 1)

                    def flip(s):
                        t = s % TT
                        pe.wait_ge(n_ready, b * NS + s + 1)
                        heads = c.hpc // 2
                        for hh in range(2):
                            if s >= 1:
                                pe.wait_ge(t_done, (b * NS + s - 1) * 2 + hh + 1)
                            for i in range(heads):
                                for k in range(c.key_tiles(t)):
                                    col = (i * c.kt + k) * P
                                    e = pe.transpose(t_ps[hh][:, col:col + P], p[:, s % 2, hh * heads + i, k * P:(k + 1) * P], ident[:, :])
                            e.then_inc(t_ready, 1)

                    def values(ch):
                        pe.wait_ge(t_done, (b * NS + ch * TT + TT) * 2)
                        bank, ready = bank_wait_free(pe, b, f"o{ch}")
                        for i in range(c.hpc):
                            for k in range(c.kt):
                                q0_ = k * P if c.causal else 0
                                e = pe.matmul(bank[i * c.m:(i + 1) * c.m, q0_:S], v[:, k, ch * c.hpc + i, :], pT[:, ch % 2, i * c.kt + k, q0_:S],
                                              start=k == 0, stop=k == c.kt - 1, skip_group_check=True)
                        e.then_inc(ready, 1)

                    scores(0)
                    scores(1)
                    for s in range(NS):
                        flip(s)
                        if s + 2 < NS:
                            scores(s + 2)
                        if s >= 2 and s % TT == 0:
                            values(s // TT - 1)
                    values(NCH - 1)
                    for u in (f"o{NCH - 2}", f"o{NCH - 1}"):
                        pe.wait_ge(a_free[at[u] % 2], b * UA + at[u] // 2 + 2)
                    bank, ready = bank_wait_free(pe, b, "out")
                    for t in range(TT):
                        o = bank[:, t * D:(t + 1) * D]
                        for ch in range(NCH):
                            pe.matmul(o, yT[:, ch, t * P:(t + 1) * P], wo[:, ch, :], start=ch == 0, stop=False)
                        e = pe.matmul(o, ones[:, :], bo[:, :], start=False, stop=True)
                    e.then_inc(ready, 1)
                    if c.cross:
                        pe.drain().then_inc(in_used, 1)

def expert_phase(nc, layer, x_res, ident, ins):
    moe0 = layer == "L0_ffn"
    n = layer
    E = 64 if moe0 else 8
    F = P if moe0 else 1024
    NF = F // P
    TB = 512
    NB = B * S // TB
    with ExitStack() as ctx:
        def sb(name, shape, dt=F32):
            return ctx.enter_context(nc.sbuf_tensor(f"{n}_{name}", shape, dt))

        def sem(name):
            return nc.alloc_semaphore(name=f"{n}_{name}")

        bank = [ctx.enter_context(nc.psum_tensor(f"{n}_bank{i}", [P, 512], F32)) for i in range(4)]
        y_ps = [ctx.enter_context(nc.psum_tensor(f"{n}_y{i}", [P, 4, D], F32)) for i in range(2)]
        zTa = sb("zTa", [P, DC, B * S])
        gate = sb("gate", [P, TILES, E])

        with ExitStack() as rctx:
            def rb(name, shape, dt=F32):
                return rctx.enter_context(nc.sbuf_tensor(f"{n}_{name}", shape, dt))
            wr = rb("wr", [P, DC, E])
            stats = rb("stats", [P, TT, 6])
            mv = rb("mv", [P, TT, 2])
            rstd = rb("rstd", [P, TT])
            eps_t = rb("eps", [P, TT])
            power = rb("power", [P, TT])
            z = rb("z", [P, TT, D])
            zT = rb("zT", [P, DC, S])
            sc = rb("sc", [P, TT, E])
            swb = rb("swb", [P, E])
            br = rb("br", [P, E])
            lower = rb("lower", [P, 8, 8])
            top = rb("top", [P, 8, 8])
            gs = rb("gs", [P, 8])
            cmp = rb("cmp", [P, 8, 8])
            eq = rb("eq", [P, 8, 8])
            rank = rb("rank", [P, 8])
            msk = rb("msk", [P, E])
            top8 = rb("top8", [P, 8])
            sel = rb("sel", [P, E])
            wsum = rb("wsum", [P, 1])
            loaded = sem("r_loaded")
            gp_set = sem("r_gp_set")
            var_ready = sem("r_var_ready")
            rstd_ready = sem("r_rstd_ready")
            z_ready = sem("r_z_ready")
            t_ready = sem("r_t_ready")
            t_act = sem("r_t_act")
            t_dve = sem("r_t_dve")
            l_ready = sem("r_l_ready")
            sc_ready = sem("r_sc_ready")
            sc_used = sem("r_sc_used")
            rloads = [(wr, "wr"), (lower, "lower")] + ([(br, "br")] if moe0 else [])
            with nc.Block() as block:
                @block.sync
                def _(sp):
                    for dst, key in rloads:
                        sp.dma_start(dst[:], ins[key]).then_inc(loaded, 16)

                @block.gpsimd
                def _(pool):
                    pool.memset(eps_t[:, :], LN_EPS).then_inc(gp_set, 1)
                    pool.memset(power[:, :], -0.5).then_inc(gp_set, 1)
                    pool.wait_ge(gp_set, 2)
                    with pool.Fori(0, B, 1) as b:
                        pool.wait_ge(var_ready, b + 1)
                        pool.tensor_tensor(mv[:, :, 1], mv[:, :, 1], eps_t[:, :], ALU.add)
                        pool.drain()
                        pool.tensor_tensor(rstd[:, :], mv[:, :, 1], power[:, :], ALU.pow).then_inc(rstd_ready, 1)

                @block.vector
                def _(dve):
                    dve.sem_inc(t_act, 1)
                    dve.sem_inc(t_dve, 1)
                    dve.sem_inc(sc_used, 1)
                    dve.wait_ge(loaded, 16 * len(rloads))
                    with dve.Fori(0, B, 1) as b:
                        for t in range(TT):
                            dve.bn_stats(stats[:, t, :], x_res[:, bass.ds(b * TT + t, 1), :])
                        dve.drain()
                        for t in range(TT):
                            e = dve.bn_aggr(mv[:, t, :], stats[:, t, :])
                        e.then_inc(var_ready, 1)
                        dve.drain()
                        dve.wait_ge(rstd_ready, b + 1)
                        for t in range(TT):
                            e = dve.tensor_scalar(z[:, t, :], x_res[:, bass.ds(b * TT + t, 1), :], mv[:, t, 0:1], rstd[:, t:t + 1], ALU.subtract, ALU.mult)
                        e.then_inc(z_ready, 1)
                        dve.wait_ge(t_act, b + 2)
                        dve.tensor_copy(zTa[:, :, bass.ds(b * S, S)], zT[:, :, :]).then_inc(t_dve, 1)
                        dve.wait_ge(sc_ready, b + 1)
                        for t in range(TT):
                            scores = sc[:, t, :]
                            if moe0:
                                dve.tensor_tensor(swb[:, :], scores, br[:, :], ALU.add)
                                dve.drain()
                                for g in range(8):
                                    dve.max(top[:, g, :], swb[:, 8 * g:8 * g + 8])
                                dve.drain()
                                dve.tensor_tensor(gs[:, :], top[:, :, 0], top[:, :, 1], ALU.add)
                                dve.drain()
                                dve.tensor_tensor(cmp[:, :, :], gs[:, None, :].to_broadcast([P, 8, 8]), gs[:, :, None].to_broadcast([P, 8, 8]), ALU.is_gt)
                                dve.tensor_tensor(eq[:, :, :], gs[:, None, :].to_broadcast([P, 8, 8]), gs[:, :, None].to_broadcast([P, 8, 8]), ALU.is_equal)
                                dve.drain()
                                dve.tensor_tensor(eq[:, :, :], eq[:, :, :], lower[:, :, :], ALU.mult)
                                dve.drain()
                                dve.tensor_tensor(cmp[:, :, :], cmp[:, :, :], eq[:, :, :], ALU.add)
                                dve.drain()
                                dve.tensor_reduce(rank[:, :], cmp[:, :, :], AX.X, ALU.add)
                                dve.drain()
                                dve.tensor_scalar(rank[:, :], rank[:, :], 4.0, None, ALU.is_lt)
                                dve.drain()
                                dve.tensor_tensor(msk[:, :].rearrange("p (g e) -> p g e", e=8), swb[:, :].rearrange("p (g e) -> p g e", e=8),
                                                  rank[:, :, None].to_broadcast([P, 8, 8]), ALU.mult)
                                dve.drain()
                                dve.max(top8[:, :], msk[:, :])
                                dve.drain()
                                dve.match_replace(sel[:, :], top8[:, :], msk[:, :], -1e30)
                                dve.drain()
                                dve.tensor_scalar(sel[:, :], sel[:, :], -1e29, None, ALU.is_lt)
                                dve.drain()
                                dve.tensor_tensor(sel[:, :], sel[:, :], scores, ALU.mult)
                                dve.drain()
                                dve.tensor_reduce(wsum[:, :], sel[:, :], AX.X, ALU.add)
                                dve.drain()
                                dve.tensor_scalar(wsum[:, :], wsum[:, :], 1e-20, None, ALU.add)
                                dve.drain()
                                dve.reciprocal(wsum[:, :], wsum[:, :])
                                dve.drain()
                                e = dve.tensor_scalar(gate[:, bass.ds(b * TT + t, 1), :], sel[:, None, :], 2.5, wsum[:, 0:1], ALU.mult, ALU.mult)
                            else:
                                dve.tensor_tensor(cmp[:, :, :], sc[:, t:t + 1, :].to_broadcast([P, 8, 8]), sc[:, t, :, None].to_broadcast([P, 8, 8]), ALU.is_gt)
                                dve.tensor_tensor(eq[:, :, :], sc[:, t:t + 1, :].to_broadcast([P, 8, 8]), sc[:, t, :, None].to_broadcast([P, 8, 8]), ALU.is_equal)
                                dve.tensor_reduce(wsum[:, :], scores, AX.X, ALU.max)
                                dve.drain()
                                dve.tensor_tensor(eq[:, :, :], eq[:, :, :], lower[:, :, :], ALU.mult)
                                dve.drain()
                                dve.tensor_tensor(cmp[:, :, :], cmp[:, :, :], eq[:, :, :], ALU.add)
                                dve.drain()
                                dve.tensor_reduce(rank[:, :], cmp[:, :, :], AX.X, ALU.add)
                                dve.drain()
                                dve.tensor_scalar(rank[:, :], rank[:, :], 2.0, LOW, ALU.is_ge, ALU.mult)
                                dve.drain()
                                dve.scalar_tensor_tensor(sel[:, :], scores, wsum[:, 0:1], rank[:, :], ALU.subtract, ALU.add)
                                dve.drain()
                                e = dve.tensor_copy(gate[:, bass.ds(b * TT + t, 1), :], sel[:, None, :])
                            dve.drain()
                        dve.drain().then_inc(sc_used, 1)

                @block.scalar
                def _(act):
                    with act.Fori(0, B, 1) as b:
                        act.wait_ge(t_ready, b + 1)
                        act.activation(zT[:, :, :], bank[0][:, :].rearrange("p (c q) -> p c q", q=S), ACT.Copy).then_inc(t_act, 1)
                        act.wait_ge(sc_used, b + 1)
                        act.wait_ge(l_ready, b + 1)
                        act.activation(sc[:, :, :], bank[1][:, 0:TT * E].rearrange("p (t e) -> p t e", e=E), ACT.Sigmoid if moe0 else ACT.Copy).then_inc(sc_ready, 1)

                @block.tensor
                def _(pe):
                    pe.wait_ge(loaded, 16 * len(rloads))
                    with pe.Fori(0, B, 1) as b:
                        pe.wait_ge(z_ready, b + 1)
                        pe.wait_ge(t_act, b + 1)
                        pe.wait_ge(t_dve, b + 1)
                        for cc in range(DC):
                            for t in range(TT):
                                e = pe.transpose(bank[0][:, cc * S + t * P:cc * S + (t + 1) * P], z[:, t, cc * P:(cc + 1) * P], ident[:, :])
                        e.then_inc(t_ready, 1)
                        pe.wait_ge(t_act, b + 2)
                        pe.wait_ge(sc_used, b + 1)
                        for t in range(TT):
                            for cc in range(DC):
                                e = pe.matmul(bank[1][:, t * E:(t + 1) * E], zT[:, cc, t * P:(t + 1) * P], wr[:, cc, :], start=cc == 0, stop=cc == DC - 1)
                        e.then_inc(l_ready, 1)

            if not moe0:
                e_done = sem("r_e_done")
                gsum = rb("gsum", [P, TILES])
                with nc.Block() as block:
                    @block.scalar
                    def _(act):
                        act.activation(gate[:, :, :], gate[:, :, :], ACT.Exp).then_inc(e_done, 1)

                    @block.vector
                    def _(dve):
                        dve.wait_ge(e_done, 1)
                        dve.tensor_reduce(gsum[:, :], gate[:, :, :], AX.X, ALU.add)
                        dve.drain()
                        dve.reciprocal(gsum[:, :], gsum[:, :])
                        dve.drain()
                        dve.tensor_tensor(gate[:, :, :], gate[:, :, :], gsum[:, :, None].to_broadcast([P, TILES, E]), ALU.mult)

        w1 = [sb(f"w1_{i}", [P, DC, 2, F] if moe0 else [P, DC, F]) for i in range(2)]
        w2 = [sb(f"w2_{i}", [P, NF, D]) for i in range(2)]
        h = sb("h", [P, 2, NF, TB])
        sg = sb("sg", [P, 2, TB]) if moe0 else None
        one = sb("one", [P, 1])
        w_in = [sem(f"w_in{i}") for i in range(2)]
        w_used = sem("w_used")
        h_ps = sem("h_ps")
        h_free = [sem(f"h_free{i}") for i in range(2)]
        sg_ready = sem("sg_ready")
        h_ready = sem("h_ready")
        y_ready = sem("y_ready")
        y_free = sem("y_free")

        HU = 1 if moe0 else NF // 2

        with nc.Block() as block:
            shared = 1 if moe0 else 0

            def wdma(sp, e, i):
                if moe0:
                    sp.dma_start(w1[i][:, :, 0, :], ins["w_gate"][bass.ds(e, 1), :, :].rearrange("e (c p) f -> p (e c) f", p=P)).then_inc(w_in[i], 16)
                    sp.dma_start(w1[i][:, :, 1, :], ins["w_up"][bass.ds(e, 1), :, :].rearrange("e (c p) f -> p (e c) f", p=P)).then_inc(w_in[i], 16)
                    sp.dma_start(w2[i][:, :, :], ins["w_down"][bass.ds(e, 1), :, :].rearrange("e p d -> p e d")).then_inc(w_in[i], 16)
                else:
                    sp.dma_start(w1[i][:, :, :], ins["w1"][bass.ds(e, 1), :, :].rearrange("e (c p) f -> p (e c) f", p=P)).then_inc(w_in[i], 16)
                    sp.dma_start(w2[i][:, :, :], ins["w2"][bass.ds(e, 1), :, :].rearrange("e (f p) d -> p (e f) d", p=P)).then_inc(w_in[i], 16)
            WD = 16 * (3 if moe0 else 2)

            @block.sync
            def _(sp):
                with sp.Fori(0, E // 2, 1) as pair:
                    for i in range(2):
                        sp.wait_ge(w_used, pair * 2 + i + 1)
                        wdma(sp, pair * 2 + i, i)
                if shared:
                    sp.wait_ge(w_used, E + 1)
                    sp.dma_start(w1[0][:, :, 0, :], ins["ws_gate"].rearrange("(c p) f -> p c f", p=P)).then_inc(w_in[0], 16)
                    sp.dma_start(w1[0][:, :, 1, :], ins["ws_up"].rearrange("(c p) f -> p c f", p=P)).then_inc(w_in[0], 16)
                    sp.dma_start(w2[0][:, 0, :], ins["ws_down"]).then_inc(w_in[0], 16)

            @block.tensor
            def _(pe):
                def hid(e, i, tb):
                    for j in range(NF):
                        if moe0:
                            pe.wait_ge(h_free[tb % 2], e * (NB // 2) + tb // 2 + 1)
                            for u in range(2):
                                for cc in range(DC):
                                    m = pe.matmul(bank[2 * (tb % 2) + u][:, :], w1[i][:, cc, u, :], zTa[:, cc, tb * TB:(tb + 1) * TB], start=cc == 0, stop=cc == DC - 1)
                        else:
                            pe.wait_ge(h_free[j % 2], (e * NB + tb) * HU + j // 2 + 1)
                            for cc in range(DC):
                                m = pe.matmul(bank[j % 4][:, :], w1[i][:, cc, j * P:(j + 1) * P], zTa[:, cc, tb * TB:(tb + 1) * TB], start=cc == 0, stop=cc == DC - 1)
                        m.then_inc(h_ps, 1)

                def down(e, i, tb):
                    pe.wait_ge(h_ready, (e * NB + tb + 1) * NF)
                    pe.wait_ge(y_free, e * NB + tb + 1)
                    for t in range(4):
                        for f in range(NF):
                            m = pe.matmul(y_ps[tb % 2][:, t, :], h[:, tb % 2, f, t * P:(t + 1) * P], w2[i][:, f, :], start=f == 0, stop=f == NF - 1)
                    m.then_inc(y_ready, 1)

                def expert(e, i):
                    for tb in range(NB):
                        hid(e, i, tb)
                        if tb >= 1:
                            down(e, i, tb - 1)
                    down(e, i, NB - 1)
                    pe.drain().then_inc(w_used, 1)

                with pe.Fori(0, E // 2, 1) as pair:
                    for i in range(2):
                        pe.wait_ge(w_in[i], pair * WD + WD)
                        expert(pair * 2 + i, i)
                if shared:
                    pe.wait_ge(w_in[0], (E // 2 + 1) * WD)
                    expert(E, 0)

            @block.scalar
            def _(act):
                def step(e, tb):
                    if moe0:
                        act.wait_ge(h_ps, e * NB + tb + 1)
                        act.wait_ge(h_free[tb % 2], e * (NB // 2) + tb // 2 + 1)
                        act.activation(sg[:, tb % 2, :], bank[2 * (tb % 2)][:, :], ACT.Silu).then_inc(sg_ready, 1)
                    else:
                        act.wait_ge(y_ready, e * NB + tb + 1)
                        for j in range(0, NF, 2):
                            act.wait_ge(h_ps, (e * NB + tb) * NF + j + 1)
                            act.activation(h[:, tb % 2, j, :], bank[j % 4][:, :], ACT.Relu).then_inc(h_ready, 1)
                            act.drain().then_inc(h_free[0], 1)

                with act.Fori(0, E // 2, 1) as pair:
                    for i in range(2):
                        for tb in range(NB):
                            step(pair * 2 + i, tb)
                if shared:
                    for tb in range(NB):
                        step(E, tb)

            @block.vector
            def _(dve):
                if moe0:
                    for q, k in ((w_used, 2), (y_free, 2), (y_ready, 2), (h_free[0], 1), (h_free[1], 1)):
                        dve.sem_inc(q, k)
                else:
                    for q, k in ((w_used, 2), (y_free, 2), (y_ready, 2), (h_free[0], 2), (h_free[1], 2)):
                        dve.sem_inc(q, k)
                dve.memset(one[:, :], 1.0)
                dve.drain()

                def step(e, tb, weight):
                    dve.wait_ge(y_ready, e * NB + tb + 1)
                    if moe0:
                        dve.wait_ge(sg_ready, e * NB + tb + 1)
                        dve.tensor_tensor(h[:, tb % 2, 0, :], sg[:, tb % 2, :], bank[2 * (tb % 2) + 1][:, :], ALU.mult).then_inc(h_ready, 1)
                        dve.drain().then_inc(h_free[tb % 2], 1)
                    else:
                        for j in range(1, NF, 2):
                            dve.wait_ge(h_ps, (e * NB + tb) * NF + j + 1)
                            dve.tensor_scalar(h[:, tb % 2, j, :], bank[j % 4][:, :], 0.0, None, ALU.max).then_inc(h_ready, 1)
                            dve.drain().then_inc(h_free[1], 1)

                def add(e, tb, weight):
                    dve.wait_ge(y_ready, e * NB + tb + 3)
                    for t in range(4):
                        tile = tb * 4 + t
                        m = dve.scalar_tensor_tensor(x_res[:, tile, :], y_ps[tb % 2][:, t, :], weight(tile), x_res[:, tile, :], ALU.mult, ALU.add)
                    dve.drain().then_inc(y_free, 1)

                def expert(e, weight):
                    for tb in range(NB):
                        step(e, tb, weight)
                        if tb >= 1:
                            add(e, tb - 1, weight)
                    add(e, NB - 1, weight)

                with dve.Fori(0, E // 2, 1) as pair:
                    for i in range(2):
                        expert(pair * 2 + i, lambda tile, i=i: gate[:, tile, bass.ds(pair * 2 + i, 1)])
                if shared:
                    expert(E, lambda tile: one[:, 0:1])

def build(nc, ins, out, stages=STAGES):
    with ExitStack() as ctx:
        x_res = ctx.enter_context(nc.sbuf_tensor("x_res", [P, TILES, D], F32))
        ident = ctx.enter_context(nc.sbuf_tensor("ident", [P, P], F32))
        x_in = nc.alloc_semaphore(name="x_in")
        x_out = nc.alloc_semaphore(name="x_out")
        with nc.Block() as block:
            @block.sync
            def _(sp):
                sp.dma_start(ident[:, :], ins["ident"]).then_inc(x_in, 16)
                sp.dma_start(x_res[:, :, :], ins["x"].rearrange("b (t p) d -> p (b t) d", p=P)).then_inc(x_in, 16)
                sp.wait_ge(x_in, 32)
        phases = ["L0_attn", "L0_xattn", "L0_ffn", "L1_attn", "L1_xattn", "L1_ffn"]
        for name in phases[:stages]:
            part = {k[len(name) + 1:]: v for k, v in ins.items() if k.startswith(name + "_")}
            part.update({k[7:]: v for k, v in ins.items() if k.startswith("shared_")})
            if name in ATTN:
                attention_phase(nc, ATTN[name], x_res, ident, part)
            else:
                expert_phase(nc, name, x_res, ident, part)
        with nc.Block() as block:
            @block.sync
            def _(sp):
                sp.dma_start(out.rearrange("b (t p) d -> p (b t) d", p=P), x_res[:, :, :]).then_inc(x_out, 16)
                sp.wait_ge(x_out, 16)

def layout(inputs):
    import numpy as np

    bf = mybir.dt.np(BF16)
    g = {k: np.asarray(v) for k, v in inputs.items()}
    a = {"ident": np.eye(P, dtype=np.float32), "x": g["x"]}

    def by_rows(wt):
        return wt.reshape(-1, P, wt.shape[1]).transpose(1, 0, 2)

    def column(v):
        return v.reshape(-1, P).T

    zeros = np.zeros(D, np.float32)
    for name, c in ATTN.items():
        w = {k: g.get(f"{name}_{k}") for k in ("Wq", "Wk", "Wv", "Wo", "bq", "bk", "bv", "bo", "Wgk", "bgk", "Wgv", "bgv")}
        for k in ("bq", "bk", "bv", "bo"):
            if w[k] is None:
                w[k] = zeros
        put = {}
        for k in "qkv":
            put["w" + k] = by_rows(w["W" + k].T)
        put["bq"], put["bk"] = column(w["bq"]), column(w["bk"])
        put["bv"], put["bo"] = w["bv"][None, :], w["bo"][None, :]
        wo = np.zeros((c.chunks, c.hpc, c.m, D), np.float32)
        wo[:, :, :c.dk, :] = w["Wo"].T.reshape(c.chunks, c.hpc, c.dk, D)
        put["wo"] = wo.reshape(c.chunks, P, D).transpose(1, 0, 2)
        if c.rope:
            half = c.dk // 2
            swap = np.arange(D).reshape(H, 2, half)[:, ::-1, :].reshape(-1)
            for k in "qk":
                put[f"w{k}r"] = by_rows(w["W" + k][swap].T)
                put[f"b{k}r"] = column(w["b" + k][swap])
            theta = 1.0 / 10000.0 ** (np.arange(0, c.dk, 2, dtype=np.float32) / np.float32(c.dk))
            theta = theta.astype(np.float32)
            ang = np.arange(1, S + 1, dtype=np.float32)[:, None] * theta[None, :]
            ang = np.concatenate([ang, ang], -1)
            sign = np.concatenate([-np.ones(half), np.ones(half)]).astype(np.float32)
            put["cos"] = np.tile(np.cos(ang).astype(np.float32).T, (P // c.dk, 1))
            put["sin"] = np.tile((np.sin(ang).astype(np.float32) * sign).T, (P // c.dk, 1))
        if c.wide:
            put["wgk"], put["wgv"] = by_rows(w["Wgk"].T), by_rows(w["Wgv"].T)
            put["bgk"], put["bgv"] = column(w["bgk"]), w["bgv"][None, :]
            put["low_ident"] = (np.eye(P) * LOW).astype(bf)
            put["mask"] = g["mask_Bx16xSxS_bk1"]
            put["src"], put["grid"] = g["fside_BxSxS_0"], g["ctx_1024"]
        else:
            put["headmask"] = (np.arange(P)[:, None] // c.dk == np.arange(8)[None, :]).astype(np.float32)
        if c.causal:
            put["ident_bf"] = np.eye(P).astype(bf)
            put["tri"] = np.where(np.arange(P)[:, None] >= np.arange(P)[None, :], 0.0, LOW).astype(bf)
        if c.keymask:
            rest, parts = MASKED, []
            for _ in range(3):
                parts.append(np.asarray(rest).astype(bf))
                rest = rest - float(parts[-1])
            put["masked3"] = np.repeat(np.array(parts)[:, None], P, 1)
            put["mask"] = g["mask_Bx1x1xS2_ik0"].reshape(B, S)
            put["src"] = g["ctx_1024"]
        a.update({f"{name}_{k}": v for k, v in put.items()})
    lower = np.broadcast_to((np.arange(8)[None, :] < np.arange(8)[:, None]).astype(np.float32), (P, 8, 8))
    a.update({
        "L0_ffn_wr": by_rows(g["L0_ffn_w_router"]), "L0_ffn_lower": lower, "L1_ffn_lower": lower,
        "L0_ffn_br": np.broadcast_to(g["L0_ffn_b_router"], (P, 64)),
        "L0_ffn_w_gate": g["L0_ffn_we_gate"], "L0_ffn_w_up": g["L0_ffn_we_up"], "L0_ffn_w_down": g["L0_ffn_we_down"],
        "L0_ffn_ws_gate": g["L0_ffn_ws_gate"], "L0_ffn_ws_up": g["L0_ffn_ws_up"], "L0_ffn_ws_down": g["L0_ffn_ws_down"],
        "L1_ffn_wr": by_rows(g["L1_ffn_gate_w"].T),
        "L1_ffn_w1": g["L1_ffn_w1"].transpose(0, 2, 1), "L1_ffn_w2": g["L1_ffn_w2"].transpose(0, 2, 1),
    })
    return {k: np.ascontiguousarray(v) for k, v in a.items()}

def kernel(**inputs):
    import numpy as np
    import concourse.bacc as bacc
    from concourse.bass_utils import run_bass_kernel_spmd

    nc = bacc.Bacc("TRN2", target_bir_lowering=False, num_devices=1)
    arrays = {f"in_{k}": v for k, v in layout(inputs).items()}
    aps = {k[3:]: nc.dram_tensor(k, v.shape, mybir.dt.from_np(v.dtype), kind="ExternalInput").ap() for k, v in arrays.items()}
    out = nc.dram_tensor("out", (B, S, D), F32, kind="ExternalOutput").ap()
    build(nc, aps, out)
    r = run_bass_kernel_spmd(nc, [arrays], core_ids=[0])
    return r.results[0]["out"]
```

```python
from contextlib import ExitStack

import concourse.bass as bass
from concourse import mybir

F32 = mybir.dt.float32
BF16 = mybir.dt.bfloat16
I32 = mybir.dt.int32
F32R = mybir.dt.float32r
ACT = mybir.ActivationFunctionType
ALU = mybir.AluOpType
AX = mybir.AxisListType

P = 128
B, S, D = 16, 256, 256
H = 16
TT = S // P
DC = D // P
TILES = B * TT
LN_EPS = 1e-5
MASKED = -1e9
LOW = -1e30
STAGES = 6

class Attn:

    def __init__(self, name, dk, keys, causal=False, rope=False, keymask=False, fullmask=False):
        self.name, self.dk, self.keys = name, dk, keys
        self.causal, self.rope, self.keymask, self.fullmask = causal, rope, keymask, fullmask
        self.cross = keymask or fullmask
        self.wide = fullmask
        self.hpc = 1024 // keys
        self.chunks = H // self.hpc
        self.steps = self.chunks * TT
        self.inner = H * dk
        self.groups = self.inner // P
        self.kt = keys // P
        self.m = P // self.hpc
        self.scale = dk ** -0.5

    def key_tiles(self, t):
        return t + 1 if self.causal else self.kt

ATTN = {
    "L0_attn": Attn("L0_attn", 16, S, causal=True),
    "L0_xattn": Attn("L0_xattn", 16, S, keymask=True),
    "L1_attn": Attn("L1_attn", 16, S, causal=True, rope=True),
    "L1_xattn": Attn("L1_xattn", 64, 2 * S, fullmask=True),
}

def tile_pair(x_res, b):
    return x_res[:, bass.ds(b * TT, TT), :]

def attention_phase(nc, c, x_res, ident, ins):
    n = c.name
    with ExitStack() as ctx:
        def sb(name, shape, dt=F32):
            return ctx.enter_context(nc.sbuf_tensor(f"{n}_{name}", shape, dt))

        def sem(name):
            return nc.alloc_semaphore(name=f"{n}_{name}")

        ps = [ctx.enter_context(nc.psum_tensor(f"{n}_bank{i}", [P, 512], F32)) for i in range(4, 8)]
        s_ps = [ctx.enter_context(nc.psum_tensor(f"{n}_scores{i}", [P, c.hpc, c.keys], F32)) for i in range(2)]
        t_ps, a_ps = ps[0:2], ps[2:4]

        wq = sb("wq", [P, DC, c.inner])
        wk = sb("wk", [P, DC, c.inner])
        wv = sb("wv", [P, DC, c.inner])
        wo = sb("wo", [P, c.chunks, D])
        bq = sb("bq", [P, c.groups])
        bk = sb("bk", [P, c.groups])
        bv = sb("bv", [P, c.inner])
        bo = sb("bo", [P, D])
        y_bias = sb("y_bias", [P, TT, D])
        loads = [(wq, "wq"), (wk, "wk"), (wv, "wv"), (wo, "wo"), (bq, "bq"), (bk, "bk"), (bv, "bv"), (bo, "bo")]
        if c.rope:
            wqr = sb("wqr", [P, DC, D])
            wkr = sb("wkr", [P, DC, D])
            bqr = sb("bqr", [P, c.groups])
            bkr = sb("bkr", [P, c.groups])
            cos = sb("cos", [P, S])
            sin = sb("sin", [P, S])
            loads += [(wqr, "wqr"), (wkr, "wkr"), (bqr, "bqr"), (bkr, "bkr"), (cos, "cos"), (sin, "sin")]
        if c.wide:
            wgk = sb("wgk", [P, DC, c.inner])
            wgv = sb("wgv", [P, DC, c.inner])
            bgk = sb("bgk", [P, c.groups])
            bgv = sb("bgv", [P, c.inner])
            loads += [(wgk, "wgk"), (wgv, "wgv"), (bgk, "bgk"), (bgv, "bgv")]
            low_ident = sb("low_ident", [P, P], BF16)
            loads += [(low_ident, "low_ident")]
        else:
            headmask = sb("headmask", [P, 8])
            loads += [(headmask, "headmask")]
        if c.causal:
            ident_bf = sb("ident_bf", [P, P], BF16)
            tri = sb("tri", [P, P], BF16)
            loads += [(ident_bf, "ident_bf"), (tri, "tri")]
        if c.keymask:
            masked3 = sb("masked3", [P, P], BF16)
            loads += [(masked3, "masked3")]

        stats = sb("stats", [P, TT, 6])
        mv = sb("mv", [P, TT, 2])
        rstd = sb("rstd", [P, TT])
        eps_t = sb("eps", [P, TT])
        power = sb("power", [P, TT])
        z = sb("z", [P, TT, D])
        zT = sb("zT", [P, DC, S])
        if c.cross:
            src = sb("src", [P, TT, D])
            srcT = sb("srcT", [P, DC, S])
        else:
            srcT = zT
        if c.wide:
            grid = sb("grid", [P, TT, D])
            gridT = sb("gridT", [P, DC, S])
            qT = sb("qT", [P, H, S])
            kT = sb("kT", [P, c.groups, c.keys])
            v = sb("v", [P, c.kt, H, c.dk])
            mask = sb("mask", [P, 4, c.hpc, S], BF16)
        else:
            qT = sb("qT", [P, c.groups, S])
            kT1 = sb("kT1", [P, c.groups, S])
            kT = sb("kT", [P, H, S])
            v = sb("v", [P, c.kt, H, c.m])
        if c.rope:
            qr = sb("qr", [P, c.groups, S])
            q0 = sb("q0", [P, c.groups, S])
            kr = sb("kr", [P, c.groups, S])
        if c.keymask:
            mask_i = sb("mask_i", [P, S], I32)
            keep = sb("keep", [P, S])
            drop = sb("drop", [P, S], BF16)
        PR = 3
        negmax = sb("negmax", [P, 2, c.hpc])
        lsum = sb("lsum", [P, 2, c.hpc])
        rsum = sb("rsum", [P, 2, c.hpc])
        p = sb("p", [P, PR, c.hpc, c.keys])
        pT = sb("pT", [P, 2, 8, S])
        yT = sb("yT", [P, c.chunks, S])

        loaded = sem("loaded")
        gp_set = sem("gp_set")
        in_loaded = sem("in_loaded")
        in_used = sem("in_used")
        z_ready = sem("z_ready")
        var_ready = sem("var_ready")
        rstd_ready = sem("rstd_ready")
        a_ready = [sem(f"a_ready{i}") for i in range(2)]
        a_free = [sem(f"a_free{i}") for i in range(2)]
        kv_ready = sem("kv_ready")
        src_k = sem("src_k")
        src_q = sem("src_q")
        s_ready = sem("s_ready")
        m_ready = sem("m_ready")
        p_ready = sem("p_ready")
        r_ready = sem("r_ready")
        n_ready = sem("n_ready")
        t_ready = sem("t_ready")
        t_done = sem("t_done")
        mask_in = [sem(f"mask_in{i}") for i in range(4)]
        keep_ready = sem("keep_ready")

        NS, NCH = c.steps, c.chunks

        uses = ["zT"]
        if c.cross:
            uses.append("srcT")
        if c.wide:
            uses.append("gridT")
        gpu = 2
        uses += [f"q{i}" for i in range(c.groups // gpu)]
        if c.rope:
            uses += ["qr"]
        if c.wide:
            uses += [f"k{i}" for i in range(c.groups)]
            uses += [f"v{i}" for i in range(2 * c.kt)]
        else:
            uses += ["k"] + (["kr"] if c.rope else []) + ["v"]
        if (len(uses) + NCH + 1) % 2:
            uses.append("pad")
        prologue = list(uses)
        uses += [f"o{i}" for i in range(NCH)] + ["out"]
        UA = len(uses) // 2
        at = {u: i for i, u in enumerate(uses)}

        def bank_wait_free(pe, b, use):
            i = at[use]
            pe.wait_ge(a_free[i % 2], b * UA + i // 2 + 1)
            return a_ps[i % 2], a_ready[i % 2]

        def bank_wait_ready(eng, b, use):
            i = at[use]
            eng.wait_ge(a_ready[i % 2], b * UA + i // 2 + 1)
            return a_ps[i % 2], a_free[i % 2]

        with nc.Block() as block:

            @block.sync
            def _(sp):
                for dst, key in loads:
                    sp.dma_start(dst[:], ins[key]).then_inc(loaded, 16)
                if c.cross:
                    with sp.Fori(0, B, 1) as b:
                        sp.wait_ge(in_used, b * 1 + 1)
                        sp.dma_start(src[:, :, :], ins["src"][bass.ds(b, 1), :, :].rearrange("b (t p) d -> p (b t) d", p=P)).then_inc(in_loaded, 16)
                        if c.wide:
                            sp.dma_start(grid[:, :, :], ins["grid"][bass.ds(b, 1), :, :].rearrange("b (t p) d -> p (b t) d", p=P)).then_inc(in_loaded, 16)
                        if c.keymask:
                            sp.dma_start(mask_i[:, :], ins["mask"][bass.ds(b, 1), :].partition_broadcast(P).rearrange("p b k -> p (b k)")).then_inc(in_loaded, 16)

            @block.gpsimd
            def _(pool):
                pool.memset(eps_t[:, :], LN_EPS).then_inc(gp_set, 1)
                pool.memset(power[:, :], -0.5).then_inc(gp_set, 1)
                if c.wide:
                    pool.memset(qT[:, :, :], 0.0).then_inc(gp_set, 1)
                else:
                    pool.memset(v[:, :, :, :], 0.0).then_inc(gp_set, 1)
                pool.wait_ge(gp_set, 3)
                pool.wait_ge(loaded, 16 * len(loads))
                with pool.Fori(0, B, 1) as b:
                    if c.wide:
                        def load_mask(s):
                            ch, t = s // TT, s % TT
                            pool.dma_start(mask[:, s % 4, :, :], ins["mask"][bass.ds(b, 1), ch * c.hpc:(ch + 1) * c.hpc, t * P:(t + 1) * P, :].rearrange("b h p k -> p (b h) k")).then_inc(mask_in[s % 4], 16)
                        pool.wait_ge(s_ready, b * NS + 1)
                        for s in range(4):
                            load_mask(s)
                    pool.wait_ge(var_ready, b + 1)
                    pool.tensor_tensor(mv[:, :, 1], mv[:, :, 1], eps_t[:, :], ALU.add)
                    pool.drain()
                    pool.tensor_tensor(rstd[:, :], mv[:, :, 1], power[:, :], ALU.pow).then_inc(rstd_ready, 1)
                    if not c.wide:
                        if c.rope:
                            for i, (a, r) in enumerate(((q0, qr), (kT1, kr))):
                                pool.wait_ge(src_k if i else src_q, b * 2 + 2)
                                pool.tensor_tensor(a[:, :, :], a[:, :, :], cos[:, None, :].to_broadcast([P, c.groups, S]), ALU.mult)
                                pool.tensor_tensor(r[:, :, :], r[:, :, :], sin[:, None, :].to_broadcast([P, c.groups, S]), ALU.mult)
                                pool.drain()
                                pool.tensor_tensor(qT[:, :, :] if i == 0 else a[:, :, :], a[:, :, :], r[:, :, :], ALU.add)
                            pool.drain()
                        else:
                            pool.wait_ge(src_k, b + 1)
                        for g in range(c.groups):
                            e = pool.tensor_tensor(kT[:, 8 * g:8 * g + 8, :], kT1[:, g:g + 1, :].to_broadcast([P, 8, S]),
                                                   headmask[:, :, None].to_broadcast([P, 8, S]), ALU.mult)
                        e.then_inc(kv_ready, 1)
                    for s in range(NS):
                        t = s % TT
                        nk = P * c.key_tiles(t)
                        if c.wide and s >= 1 and s + 3 < NS:
                            pool.wait_ge(s_ready, b * NS + s + 1)
                            load_mask(s + 3)
                        pool.wait_ge(r_ready, b * NS + s + 1)
                        pool.tensor_tensor(p[:, s % PR, :, 0:nk], p[:, s % PR, :, 0:nk],
                                           rsum[:, s % 2, :, None].to_broadcast([P, c.hpc, nk]), ALU.mult).then_inc(n_ready, 1)

            @block.vector
            def _(dve):
                for k in range(2):
                    dve.sem_inc(a_free[k], 1)
                if c.wide:
                    dve.sem_inc(s_ready, 1)
                if c.cross:
                    dve.sem_inc(in_used, 1)
                dve.wait_ge(loaded, 16 * len(loads))
                dve.wait_ge(gp_set, 3)
                with dve.Fori(0, B, 1) as b:
                    for t in range(TT):
                        dve.bn_stats(stats[:, t, :], x_res[:, bass.ds(b * TT + t, 1), :])
                    dve.drain()
                    for t in range(TT):
                        e = dve.bn_aggr(mv[:, t, :], stats[:, t, :])
                    e.then_inc(var_ready, 1)
                    dve.drain()
                    dve.wait_ge(rstd_ready, b + 1)
                    for t in range(TT):
                        e = dve.tensor_scalar(z[:, t, :], x_res[:, bass.ds(b * TT + t, 1), :], mv[:, t, 0:1], rstd[:, t:t + 1], ALU.subtract, ALU.mult)
                    e.then_inc(z_ready, 1)
                    if c.keymask:
                        dve.wait_ge(in_loaded, b * 32 + 32)
                        dve.tensor_scalar(keep[:, :], mask_i[:, :], 0, None, ALU.not_equal)
                        dve.tensor_scalar(drop[:, :], mask_i[:, :], 0, None, ALU.is_equal).then_inc(keep_ready, 1)
                    for i in range(c.groups // gpu):
                        bank, free = bank_wait_ready(dve, b, f"q{i}")
                        for j in range(gpu):
                            g = i * gpu + j
                            if c.wide:
                                for r in range(2):
                                    rows = slice(64 * r, 64 * r + 64)
                                    e = dve.tensor_scalar(qT[rows, 2 * g + r, :], bank[rows, j * S:(j + 1) * S], bq[rows, g:g + 1], c.scale, ALU.add, ALU.mult)
                            else:
                                e = dve.tensor_scalar((q0 if c.rope else qT)[:, g, :], bank[:, j * S:(j + 1) * S], bq[:, g:g + 1], c.scale, ALU.add, ALU.mult)
                        e.then_inc(free, 1)
                        if c.rope:
                            dve.drain().then_inc(src_q, 1)
                            bank, free = bank_wait_ready(dve, b, "qr")
                            for g in range(c.groups):
                                e = dve.tensor_scalar(qr[:, g, :], bank[:, g * S:(g + 1) * S], bqr[:, g:g + 1], c.scale, ALU.add, ALU.mult)
                            e.then_inc(free, 1)
                            dve.drain().then_inc(src_q, 1)
                    if c.keymask:
                        dve.drain()
                        bank, free = bank_wait_ready(dve, b, "k")
                        for g in range(c.groups):
                            e = dve.scalar_tensor_tensor(kT1[:, g, :], bank[:, g * S:(g + 1) * S], bk[:, g:g + 1], keep[:, :], ALU.add, ALU.mult)
                        e.then_inc(free, 1)
                        dve.drain().then_inc(src_k, 1)

                    for u in prologue:
                        if u[0] != "v":
                            continue
                        bank, free = bank_wait_ready(dve, b, u)
                        if c.wide:
                            i = int(u[1:])
                            cols = slice((i % 2) * 512, (i % 2) * 512 + 512)
                            bias = (bv if i // 2 < TT else bgv)[:, cols]
                            e = dve.tensor_tensor(v[:, i // 2, 8 * (i % 2):8 * (i % 2) + 8, :], bank[:, :].rearrange("p (h d) -> p h d", d=c.dk),
                                                  bias.rearrange("p (h d) -> p h d", d=c.dk), ALU.add)
                        else:
                            for t in range(TT):
                                e = dve.tensor_tensor(v[:, t, :, 0:c.dk], bank[:, t * D:(t + 1) * D].rearrange("p (h d) -> p h d", d=c.dk),
                                                      bv[:, :].rearrange("p (h d) -> p h d", d=c.dk), ALU.add)
                        e.then_inc(free, 1)

                    def row_max(s):
                        t = s % TT
                        nk = P * c.key_tiles(t)
                        dve.wait_ge(s_ready, b * NS + s + 1 + int(c.wide))
                        dve.tensor_reduce(negmax[:, s % 2, :], s_ps[s % 2][:, :, 0:nk], AX.X, ALU.max, negate=True).then_inc(m_ready, 1)

                    def copy_flipped(s):
                        ch, t = s // TT, s % TT
                        for hh in range(2):
                            dve.wait_ge(t_ready, (b * NS + s) * 2 + hh + 1)
                            dst = pT[:, ch % 2, 4 * hh:4 * hh + 4, t * P:(t + 1) * P]
                            view = t_ps[hh][:, :].rearrange("p (a q) -> p a q", q=P)
                            if c.key_tiles(t) == 1:
                                dst = pT[:, ch % 2, 4 * hh:4 * hh + 3:2, t * P:(t + 1) * P]
                                view = view[:, 0:3:2, :]
                            dve.tensor_copy(dst, view).then_inc(t_done, 1)

                    row_max(0)
                    row_max(1)
                    for s in range(NS):
                        dve.wait_ge(p_ready, b * NS + s + 1)
                        dve.reciprocal(rsum[:, s % 2, :], lsum[:, s % 2, :]).then_inc(r_ready, 1)
                        if s + 2 < NS:
                            row_max(s + 2)
                        if s >= 1:
                            copy_flipped(s - 1)
                    copy_flipped(NS - 1)
                    bank, free = bank_wait_ready(dve, b, "out")
                    dve.tensor_tensor(y_bias[:, :, :], bank[:, :].rearrange("p (t d) -> p t d", d=D), bo[:, None, :].to_broadcast([P, TT, D]), ALU.add).then_inc(free, 1)
                    dve.drain()
                    dve.tensor_tensor(tile_pair(x_res, b), y_bias[:, :, :], tile_pair(x_res, b), ALU.add)
                    dve.drain()

            @block.scalar
            def _(act):
                act.wait_ge(loaded, 16 * len(loads))
                act.wait_ge(gp_set, 3)
                with act.Fori(0, B, 1) as b:
                    def copy_out(use, pieces):
                        bank, free = bank_wait_ready(act, b, use)
                        for dst, src_ap, bias in pieces(bank):
                            if bias is None:
                                e = act.activation(dst, src_ap, ACT.Copy)
                            else:
                                e = act.activation(dst, src_ap, ACT.Identity, bias=bias)
                        e.then_inc(free, 1)
                        return e

                    def half(bank, j):
                        return bank[:, j * S:(j + 1) * S]

                    for u in prologue:
                        if u in ("zT", "srcT", "gridT"):
                            dst = {"zT": zT, "srcT": srcT}.get(u) if u != "gridT" else gridT
                            copy_out(u, lambda bank: [(dst[:, :, :], bank[:, :].rearrange("p (c q) -> p c q", q=S), None)])
                        elif u == "k" and not c.keymask:
                            copy_out(u, lambda bank: [(kT1[:, g, :], half(bank, g), bk[:, g:g + 1]) for g in range(c.groups)])
                            act.drain().then_inc(src_k, 1)
                        elif u == "kr":
                            copy_out(u, lambda bank: [(kr[:, g, :], half(bank, g), bkr[:, g:g + 1]) for g in range(c.groups)])
                            act.drain().then_inc(src_k, 1)
                        elif u == "pad":
                            copy_out(u, lambda bank: [(yT[0:1, 0, 0:1], bank[0:1, 0:1], None)])
                        elif c.wide and u[0] == "k":
                            g = int(u[1:])
                            copy_out(u, lambda bank: [(kT[:, g, 0:S], half(bank, 0), bk[:, g:g + 1]), (kT[:, g, S:2 * S], half(bank, 1), bgk[:, g:g + 1])])
                    def copy_output(ch):
                        copy_out(f"o{ch}", lambda bank: [(yT[:, ch, :], half(bank, 0), None)])

                    for s in range(NS):
                        t = s % TT
                        nk = P * c.key_tiles(t)
                        act.wait_ge(m_ready, b * NS + s + 1)
                        if s >= PR:
                            act.wait_ge(t_ready, (b * NS + s - PR + 1) * 2)
                        for i in range(c.hpc):
                            e = act.activation(p[:, s % PR, i, 0:nk], s_ps[s % 2][:, i, 0:nk], ACT.Exp, bias=negmax[:, s % 2, i:i + 1], accum_out=lsum[:, s % 2, i:i + 1])
                        e.then_inc(p_ready, 1)
                        if s >= 5 and s % TT == 1:
                            copy_output((s - 5) // TT)
                    for ch in range((NS - 6) // TT + 1, NCH):
                        copy_output(ch)

            @block.tensor
            def _(pe):
                pe.wait_ge(loaded, 16 * len(loads))
                pe.wait_ge(gp_set, 3)
                with pe.Fori(0, B, 1) as b:
                    def transposes(use, tiles):
                        bank, ready = bank_wait_free(pe, b, use)
                        for cc in range(DC):
                            for t in range(TT):
                                e = pe.transpose(bank[:, cc * S + t * P:cc * S + (t + 1) * P], tiles[:, t, cc * P:(cc + 1) * P], ident[:, :])
                        e.then_inc(ready, 1)

                    def project(out, w, g, xT):
                        for cc in range(DC):
                            e = pe.matmul(out, w[:, cc, g * P:(g + 1) * P], xT[:, cc, :], start=cc == 0, stop=cc == DC - 1)
                        return e

                    def project_rows(out, xT, t, w, c0, cols):
                        for cc in range(DC):
                            e = pe.matmul(out, xT[:, cc, t * P:(t + 1) * P], w[:, cc, c0:c0 + cols], start=cc == 0, stop=cc == DC - 1)
                        return e

                    for u in prologue:
                        if u == "zT":
                            pe.wait_ge(z_ready, b + 1)
                            transposes("zT", z)
                        elif u == "srcT":
                            per = 16 * (1 + int(c.wide) + int(c.keymask))
                            pe.wait_ge(in_loaded, b * per + per)
                            transposes("srcT", src)
                        elif u == "gridT":
                            transposes("gridT", grid)
                        elif u == "pad":
                            bank, ready = bank_wait_free(pe, b, u)
                            pe.matmul(bank[:, 0:P], ident[:, :], ident[:, :], start=True, stop=True).then_inc(ready, 1)
                        else:
                            if u == "q0":
                                for last in ("zT", "srcT", "gridT")[:1 + int(c.cross) + int(c.wide)]:
                                    pe.wait_ge(a_free[at[last] % 2], b * UA + at[last] // 2 + 2)
                            bank, ready = bank_wait_free(pe, b, u)
                            if u[0] == "q":
                                w = wqr if u == "qr" else wq
                                i = 0 if u == "qr" else int(u[1:])
                                for j in range(gpu):
                                    e = project(bank[:, j * S:(j + 1) * S], w, i * gpu + j, zT)
                            elif u in ("k", "kr"):
                                for g in range(c.groups):
                                    e = project(bank[:, g * S:(g + 1) * S], wk if u == "k" else wkr, g, srcT)
                            elif u == "v":
                                for t in range(TT):
                                    e = project_rows(bank[:, t * D:(t + 1) * D], srcT, t, wv, 0, D)
                            elif u[0] == "k":
                                g = int(u[1:])
                                project(bank[:, 0:S], wk, g, srcT)
                                e = project(bank[:, S:2 * S], wgk, g, gridT)
                            else:
                                i = int(u[1:])
                                kt, cols = i // 2, 512
                                own = kt < TT
                                e = project_rows(bank[:, :], srcT if own else gridT, kt % TT, wv if own else wgv, (i % 2) * cols, cols)
                            e.then_inc(ready, 1)
                    for u in prologue[-2:]:
                        pe.wait_ge(a_free[at[u] % 2], b * UA + at[u] // 2 + 2)
                    if not c.wide:
                        pe.wait_ge(kv_ready, b + 1)
                    if c.keymask:
                        pe.wait_ge(keep_ready, b + 1)

                    def scores(s):
                        ch, t = s // TT, s % TT
                        nk = P * c.key_tiles(t)
                        out = s_ps[s % 2]
                        if s >= 2:
                            pe.wait_ge(p_ready, b * NS + s - 1)
                        q0_, q1_ = t * P, (t + 1) * P
                        if c.wide:
                            pe.wait_ge(mask_in[s % 4], (b * (NS // 4) + s // 4) * 16 + 16)
                            for i in range(c.hpc):
                                pe.matmul(out[:, i, :], qT[:, ch * c.hpc + i, q0_:q1_], kT[:, ch, :], start=True, stop=False, skip_group_check=True)
                                e = pe.matmul(out[:, i, 0:S], low_ident[:, :], mask[:, s % 4, i, :], start=False, stop=True, skip_group_check=True)
                        else:
                            g = ch // 2
                            for hh in range(2):
                                h0 = ch * 4 + hh * 2
                                o = out[:, 2 * hh:2 * hh + 2, 0:nk]
                                e = pe.matmul(o, qT[:, g, q0_:q1_], kT[:, h0:h0 + 2, 0:nk], start=True, stop=not (c.causal or c.keymask), skip_group_check=True)
                                if c.causal:
                                    e = pe.matmul(out[:, 2 * hh:2 * hh + 2, q0_:q1_], ident_bf[:, :], tri[:, None, :].to_broadcast([P, 2, P]), start=False, stop=True, skip_group_check=True)
                                if c.keymask:
                                    e = pe.matmul(o, masked3[:, :], drop[:, None, :].to_broadcast([P, 2, S]), start=False, stop=True, skip_group_check=True)
                        e.then_inc(s_ready, 1)

                    def flip(s):
                        t = s % TT
                        pe.wait_ge(n_ready, b * NS + s + 1)
                        heads = c.hpc // 2
                        for hh in range(2):
                            if s >= 1:
                                pe.wait_ge(t_done, (b * NS + s - 1) * 2 + hh + 1)
                            for i in range(heads):
                                for k in range(c.key_tiles(t)):
                                    col = (i * c.kt + k) * P
                                    e = pe.transpose(t_ps[hh][:, col:col + P], p[:, s % PR, hh * heads + i, k * P:(k + 1) * P], ident[:, :])
                            e.then_inc(t_ready, 1)

                    def values(ch):
                        pe.wait_ge(t_done, (b * NS + ch * TT + TT) * 2)
                        bank, ready = bank_wait_free(pe, b, f"o{ch}")
                        for i in range(c.hpc):
                            for k in range(c.kt):
                                q0_ = k * P if c.causal else 0
                                e = pe.matmul(bank[i * c.m:(i + 1) * c.m, q0_:S], v[:, k, ch * c.hpc + i, :], pT[:, ch % 2, i * c.kt + k, q0_:S],
                                              start=k == 0, stop=k == c.kt - 1, skip_group_check=True)
                        e.then_inc(ready, 1)

                    scores(0)
                    scores(1)
                    for s in range(NS + 1):
                        if s + 2 < NS:
                            scores(s + 2)
                        if s >= 1:
                            flip(s - 1)
                        if s >= 3 and s % TT == 1:
                            values((s - 3) // TT)
                    values(NCH - 1)
                    for u in (f"o{NCH - 2}", f"o{NCH - 1}"):
                        pe.wait_ge(a_free[at[u] % 2], b * UA + at[u] // 2 + 2)
                    bank, ready = bank_wait_free(pe, b, "out")
                    for t in range(TT):
                        o = bank[:, t * D:(t + 1) * D]
                        for ch in range(NCH):
                            e = pe.matmul(o, yT[:, ch, t * P:(t + 1) * P], wo[:, ch, :], start=ch == 0, stop=ch == NCH - 1)
                    e.then_inc(ready, 1)
                    if c.cross:
                        pe.drain().then_inc(in_used, 1)

def expert_phase(nc, layer, x_res, ident, ins):
    moe0 = layer == "L0_ffn"
    n = layer
    E = 64 if moe0 else 8
    F = P if moe0 else 1024
    NF = F // P
    SH = 1 if moe0 else 0
    TB = 512 if moe0 else 256
    NB = B * S // TB
    with ExitStack() as ctx:
        def sb(name, shape, dt=F32):
            return ctx.enter_context(nc.sbuf_tensor(f"{n}_{name}", shape, dt))

        def sem(name):
            return nc.alloc_semaphore(name=f"{n}_{name}")

        bank = [ctx.enter_context(nc.psum_tensor(f"{n}_bank{i}", [P, 512], F32)) for i in range(4)]
        y_ps = [ctx.enter_context(nc.psum_tensor(f"{n}_y{i}", [P, TB // P, D], F32)) for i in range(2)]
        z_hi = sb("z_hi", [P, DC, B * S], F32R)
        z_lo = sb("z_lo", [P, DC, B * S], F32R)
        gate = sb("gate", [P, TILES, SH + E])

        with ExitStack() as rctx:
            def rb(name, shape, dt=F32):
                return rctx.enter_context(nc.sbuf_tensor(f"{n}_{name}", shape, dt))
            wr = rb("wr", [P, DC, E])
            stats = rb("stats", [P, TT, 6])
            mv = rb("mv", [P, TT, 2])
            rstd = rb("rstd", [P, TT])
            eps_t = rb("eps", [P, TT])
            power = rb("power", [P, TT])
            z = rb("z", [P, TT, D])
            zT = rb("zT", [P, DC, S])
            sc = rb("sc", [P, TT, E])
            swb = rb("swb", [P, E])
            br = rb("br", [P, E])
            lower = rb("lower", [P, 8, 8])
            top = rb("top", [P, 8, 8])
            gs = rb("gs", [P, 8])
            cmp = rb("cmp", [P, 8, 8])
            eq = rb("eq", [P, 8, 8])
            rank = rb("rank", [P, 8])
            msk = rb("msk", [P, E])
            top8 = rb("top8", [P, 8])
            sel = rb("sel", [P, E])
            wsum = rb("wsum", [P, 1])
            loaded = sem("r_loaded")
            gp_set = sem("r_gp_set")
            var_ready = sem("r_var_ready")
            rstd_ready = sem("r_rstd_ready")
            z_ready = sem("r_z_ready")
            t_ready = sem("r_t_ready")
            t_act = sem("r_t_act")
            t_dve = sem("r_t_dve")
            l_ready = sem("r_l_ready")
            sc_ready = sem("r_sc_ready")
            sc_used = sem("r_sc_used")
            rloads = [(wr, "wr"), (lower, "lower")] + ([(br, "br")] if moe0 else [])
            with nc.Block() as block:
                @block.sync
                def _(sp):
                    for dst, key in rloads:
                        sp.dma_start(dst[:], ins[key]).then_inc(loaded, 16)

                @block.gpsimd
                def _(pool):
                    pool.memset(eps_t[:, :], LN_EPS).then_inc(gp_set, 1)
                    pool.memset(power[:, :], -0.5).then_inc(gp_set, 1)
                    pool.wait_ge(gp_set, 2)
                    with pool.Fori(0, B, 1) as b:
                        pool.wait_ge(var_ready, b + 1)
                        pool.tensor_tensor(mv[:, :, 1], mv[:, :, 1], eps_t[:, :], ALU.add)
                        pool.drain()
                        pool.tensor_tensor(rstd[:, :], mv[:, :, 1], power[:, :], ALU.pow).then_inc(rstd_ready, 1)

                @block.vector
                def _(dve):
                    dve.sem_inc(t_act, 1)
                    dve.sem_inc(t_dve, 1)
                    dve.sem_inc(sc_used, 1)
                    if SH:
                        dve.memset(gate[:, :, 0:1], 1.0)
                    dve.wait_ge(loaded, 16 * len(rloads))
                    with dve.Fori(0, B, 1) as b:
                        for t in range(TT):
                            dve.bn_stats(stats[:, t, :], x_res[:, bass.ds(b * TT + t, 1), :])
                        dve.drain()
                        for t in range(TT):
                            e = dve.bn_aggr(mv[:, t, :], stats[:, t, :])
                        e.then_inc(var_ready, 1)
                        dve.drain()
                        dve.wait_ge(rstd_ready, b + 1)
                        for t in range(TT):
                            e = dve.tensor_scalar(z[:, t, :], x_res[:, bass.ds(b * TT + t, 1), :], mv[:, t, 0:1], rstd[:, t:t + 1], ALU.subtract, ALU.mult)
                        e.then_inc(z_ready, 1)
                        dve.wait_ge(t_act, b + 2)
                        dve.tensor_copy(z_hi[:, :, bass.ds(b * S, S)], zT[:, :, :])
                        dve.drain()
                        dve.tensor_tensor(z_lo[:, :, bass.ds(b * S, S)], zT[:, :, :], z_hi[:, :, bass.ds(b * S, S)].bitcast(F32), ALU.subtract).then_inc(t_dve, 1)
                        dve.wait_ge(sc_ready, b + 1)
                        for t in range(TT):
                            scores = sc[:, t, :]
                            if moe0:
                                dve.tensor_tensor(swb[:, :], scores, br[:, :], ALU.add)
                                dve.drain()
                                for g in range(8):
                                    dve.max(top[:, g, :], swb[:, 8 * g:8 * g + 8])
                                dve.drain()
                                dve.tensor_tensor(gs[:, :], top[:, :, 0], top[:, :, 1], ALU.add)
                                dve.drain()
                                dve.tensor_tensor(cmp[:, :, :], gs[:, None, :].to_broadcast([P, 8, 8]), gs[:, :, None].to_broadcast([P, 8, 8]), ALU.is_gt)
                                dve.tensor_tensor(eq[:, :, :], gs[:, None, :].to_broadcast([P, 8, 8]), gs[:, :, None].to_broadcast([P, 8, 8]), ALU.is_equal)
                                dve.drain()
                                dve.tensor_tensor(eq[:, :, :], eq[:, :, :], lower[:, :, :], ALU.mult)
                                dve.drain()
                                dve.tensor_tensor(cmp[:, :, :], cmp[:, :, :], eq[:, :, :], ALU.add)
                                dve.drain()
                                dve.tensor_reduce(rank[:, :], cmp[:, :, :], AX.X, ALU.add)
                                dve.drain()
                                dve.tensor_scalar(rank[:, :], rank[:, :], 4.0, None, ALU.is_lt)
                                dve.drain()
                                dve.tensor_tensor(msk[:, :].rearrange("p (g e) -> p g e", e=8), swb[:, :].rearrange("p (g e) -> p g e", e=8),
                                                  rank[:, :, None].to_broadcast([P, 8, 8]), ALU.mult)
                                dve.drain()
                                dve.max(top8[:, :], msk[:, :])
                                dve.drain()
                                dve.match_replace(sel[:, :], top8[:, :], msk[:, :], -1e30)
                                dve.drain()
                                dve.tensor_scalar(sel[:, :], sel[:, :], -1e29, None, ALU.is_lt)
                                dve.drain()
                                dve.tensor_tensor(sel[:, :], sel[:, :], scores, ALU.mult)
                                dve.drain()
                                dve.tensor_reduce(wsum[:, :], sel[:, :], AX.X, ALU.add)
                                dve.drain()
                                dve.tensor_scalar(wsum[:, :], wsum[:, :], 1e-20, None, ALU.add)
                                dve.drain()
                                dve.reciprocal(wsum[:, :], wsum[:, :])
                                dve.drain()
                                e = dve.tensor_scalar(gate[:, bass.ds(b * TT + t, 1), SH:], sel[:, None, :], 2.5, wsum[:, 0:1], ALU.mult, ALU.mult)
                            else:
                                dve.tensor_tensor(cmp[:, :, :], sc[:, t:t + 1, :].to_broadcast([P, 8, 8]), sc[:, t, :, None].to_broadcast([P, 8, 8]), ALU.is_gt)
                                dve.tensor_tensor(eq[:, :, :], sc[:, t:t + 1, :].to_broadcast([P, 8, 8]), sc[:, t, :, None].to_broadcast([P, 8, 8]), ALU.is_equal)
                                dve.tensor_reduce(wsum[:, :], scores, AX.X, ALU.max)
                                dve.drain()
                                dve.tensor_tensor(eq[:, :, :], eq[:, :, :], lower[:, :, :], ALU.mult)
                                dve.drain()
                                dve.tensor_tensor(cmp[:, :, :], cmp[:, :, :], eq[:, :, :], ALU.add)
                                dve.drain()
                                dve.tensor_reduce(rank[:, :], cmp[:, :, :], AX.X, ALU.add)
                                dve.drain()
                                dve.tensor_scalar(rank[:, :], rank[:, :], 2.0, LOW, ALU.is_ge, ALU.mult)
                                dve.drain()
                                dve.scalar_tensor_tensor(sel[:, :], scores, wsum[:, 0:1], rank[:, :], ALU.subtract, ALU.add)
                                dve.drain()
                                e = dve.tensor_copy(gate[:, bass.ds(b * TT + t, 1), :], sel[:, None, :])
                            dve.drain()
                        dve.drain().then_inc(sc_used, 1)

                @block.scalar
                def _(act):
                    with act.Fori(0, B, 1) as b:
                        act.wait_ge(t_ready, b + 1)
                        act.activation(zT[:, :, :], bank[0][:, :].rearrange("p (c q) -> p c q", q=S), ACT.Copy).then_inc(t_act, 1)
                        act.wait_ge(sc_used, b + 1)
                        act.wait_ge(l_ready, b + 1)
                        act.activation(sc[:, :, :], bank[1][:, 0:TT * E].rearrange("p (t e) -> p t e", e=E), ACT.Sigmoid if moe0 else ACT.Copy).then_inc(sc_ready, 1)

                @block.tensor
                def _(pe):
                    pe.wait_ge(loaded, 16 * len(rloads))
                    with pe.Fori(0, B, 1) as b:
                        pe.wait_ge(z_ready, b + 1)
                        pe.wait_ge(t_act, b + 1)
                        pe.wait_ge(t_dve, b + 1)
                        for cc in range(DC):
                            for t in range(TT):
                                e = pe.transpose(bank[0][:, cc * S + t * P:cc * S + (t + 1) * P], z[:, t, cc * P:(cc + 1) * P], ident[:, :])
                        e.then_inc(t_ready, 1)
                        pe.wait_ge(t_act, b + 2)
                        pe.wait_ge(sc_used, b + 1)
                        for t in range(TT):
                            for cc in range(DC):
                                e = pe.matmul(bank[1][:, t * E:(t + 1) * E], zT[:, cc, t * P:(t + 1) * P], wr[:, cc, :], start=cc == 0, stop=cc == DC - 1)
                        e.then_inc(l_ready, 1)

            if not moe0:
                e_done = sem("r_e_done")
                gsum = rb("gsum", [P, TILES])
                with nc.Block() as block:
                    @block.scalar
                    def _(act):
                        act.activation(gate[:, :, :], gate[:, :, :], ACT.Exp).then_inc(e_done, 1)

                    @block.vector
                    def _(dve):
                        dve.wait_ge(e_done, 1)
                        dve.tensor_reduce(gsum[:, :], gate[:, :, :], AX.X, ALU.add)
                        dve.drain()
                        dve.reciprocal(gsum[:, :], gsum[:, :])
                        dve.drain()
                        dve.tensor_tensor(gate[:, :, :], gate[:, :, :], gsum[:, :, None].to_broadcast([P, TILES, E]), ALU.mult)

        R = 2 if moe0 else 1
        W1 = 2 * F if moe0 else F
        NU = 1 if moe0 else F * TB // (P * 512)
        TY = TB // P
        LAST = SH + E - 1
        raw1 = sb("raw1", [P, DC, W1])
        raw2 = sb("raw2", [P, NF, D])
        w1_hi = [sb(f"w1_hi{i}", [P, DC, W1], F32R) for i in range(R)]
        w1_lo = [sb(f"w1_lo{i}", [P, DC, W1], F32R) for i in range(R)]
        w2_hi = [sb(f"w2_hi{i}", [P, NF, D], F32R) for i in range(R)]
        w2_lo = [sb(f"w2_lo{i}", [P, NF, D], F32R) for i in range(R)]
        hf = sb("hf", [P, 2, NU, 512])
        h_hi = [sb(f"h_hi{i}", [P, NU * 512], F32R) for i in range(2)]
        h_lo = [sb(f"h_lo{i}", [P, NU * 512], F32R) for i in range(2)]
        sg = sb("sg", [P, 2, 512]) if moe0 else None
        w_in = sem("w_in")
        w_hi = sem("w_hi")
        w_ready = sem("w_ready")
        w_used = sem("w_used")
        h_ps = sem("h_ps")
        sg_ready = sem("sg_ready")
        U0 = 2 if moe0 else 4
        hf_ready = sem("hf_ready")
        h_ready = sem("h_ready")
        y_ready = sem("y_ready")
        y_free = sem("y_free")
        WD = 16 * (3 if moe0 else 2)

        with nc.Block() as block:

            def place(k):
                return k % R

            @block.sync
            def _(sp):
                if SH:
                    sp.wait_ge(w_ready, 1)
                    sp.dma_start(raw1[:, :, 0:F], ins["ws_gate"].rearrange("(c p) f -> p c f", p=P)).then_inc(w_in, 16)
                    sp.dma_start(raw1[:, :, F:2 * F], ins["ws_up"].rearrange("(c p) f -> p c f", p=P)).then_inc(w_in, 16)
                    sp.dma_start(raw2[:, 0, :], ins["ws_down"]).then_inc(w_in, 16)
                with sp.Fori(0, E, 1) as e:
                    sp.wait_ge(w_ready, e + SH + 1)
                    if moe0:
                        sp.dma_start(raw1[:, :, 0:F], ins["w_gate"][bass.ds(e, 1), :, :].rearrange("e (c p) f -> p (e c) f", p=P)).then_inc(w_in, 16)
                        sp.dma_start(raw1[:, :, F:2 * F], ins["w_up"][bass.ds(e, 1), :, :].rearrange("e (c p) f -> p (e c) f", p=P)).then_inc(w_in, 16)
                        sp.dma_start(raw2[:, :, :], ins["w_down"][bass.ds(e, 1), :, :].rearrange("e p d -> p e d")).then_inc(w_in, 16)
                    else:
                        sp.dma_start(raw1[:, :, :], ins["w1"][bass.ds(e, 1), :, :].rearrange("e (c p) f -> p (e c) f", p=P)).then_inc(w_in, 16)
                        sp.dma_start(raw2[:, :, :], ins["w2"][bass.ds(e, 1), :, :].rearrange("e (f p) d -> p (e f) d", p=P)).then_inc(w_in, 16)

            def over_experts(eng, body):
                if moe0:
                    body(0, 0, False)
                    with eng.Fori(0, E // 2 - 1, 1) as pair:
                        body(pair * 2 + 1, 1, False)
                        body(pair * 2 + 2, 0, False)
                    body(E - 1, 1, False)
                    body(E, 0, True)
                else:
                    with eng.Fori(0, E, 1) as e:
                        body(e, 0, False)

            @block.tensor
            def _(pe):
                def three(out, a_hi, a_lo, b_hi, b_lo, first, last):
                    pe.matmul(out, a_lo, b_hi, start=first, stop=False, skip_group_check=True)
                    pe.matmul(out, a_hi, b_lo, start=False, stop=False, skip_group_check=True)
                    return pe.matmul(out, a_hi, b_hi, start=False, stop=last, skip_group_check=True)

                def hidden(e, i, tb):
                    cols = slice(tb * TB, (tb + 1) * TB)
                    for j in range(NU):
                        pe.wait_ge(hf_ready, (e * NB + tb) * NU + j + 1)
                        for u in range(2):
                            out = bank[2 * (tb % 2) + u][:, :] if moe0 else bank[j][:, u * TB:(u + 1) * TB]
                            rows = slice((2 * j + u) * P, (2 * j + u + 1) * P)
                            for cc in range(DC):
                                m = three(out, w1_hi[i][:, cc, rows], w1_lo[i][:, cc, rows], z_hi[:, cc, cols], z_lo[:, cc, cols], cc == 0, cc == DC - 1)
                        m.then_inc(h_ps, 1)

                def down(e, i, tb):
                    pe.wait_ge(h_ready, (e * NB + tb + 1) * NU)
                    pe.wait_ge(y_free, e * NB + tb + 1)
                    for t in range(TY):
                        for f in range(NF):
                            cols = slice(f * TB + t * P, f * TB + (t + 1) * P)
                            m = three(y_ps[tb % 2][:, t, :], h_hi[tb % 2][:, cols], h_lo[tb % 2][:, cols], w2_hi[i][:, f, :], w2_lo[i][:, f, :], f == 0, f == NF - 1)
                    m.then_inc(y_ready, 1)

                def body(e, i, last):
                    pe.wait_ge(w_ready, e + 2)
                    for tb in range(NB):
                        hidden(e, i, tb)
                        if tb >= 1:
                            down(e, i, tb - 1)
                        elif moe0 and not (isinstance(e, int) and e == 0):
                            down(e - 1, 1 - i, NB - 1)
                            pe.drain().then_inc(w_used, 1)
                    if last or not moe0:
                        down(e, i, NB - 1)
                        pe.drain().then_inc(w_used, 1)

                over_experts(pe, body)

            @block.scalar
            def _(act):
                def split_high(e, i):
                    act.wait_ge(w_in, e * WD + WD)
                    act.wait_ge(w_used, e + 1)
                    act.activation(w1_hi[i][:, :, :], raw1[:, :, :], ACT.Copy)
                    act.activation(w2_hi[i][:, :, :], raw2[:, :, :], ACT.Copy).then_inc(w_hi, 1)

                def body(e, i, last):
                    if not moe0:
                        split_high(e, i)
                    for tb in range(NB):
                        if moe0:
                            act.wait_ge(h_ps, e * NB + tb + 1)
                            act.wait_ge(hf_ready, e * NB + tb + 1)
                            act.activation(sg[:, tb % 2, :], bank[2 * (tb % 2)][:, :], ACT.Silu).then_inc(sg_ready, 1)
                            if tb == 1 and not last:
                                split_high(e + 1, 1 - i)
                        else:
                            act.wait_ge(y_ready, e * NB + tb + 1)
                            for j in range(NU):
                                act.wait_ge(h_ps, (e * NB + tb) * NU + j + 1)
                                act.activation(hf[:, tb % 2, j, :], bank[j][:, :], ACT.Relu)
                                act.activation(h_hi[tb % 2][:, j * 512:(j + 1) * 512], bank[j][:, :], ACT.Relu).then_inc(hf_ready, 1)

                if moe0:
                    split_high(0, 0)
                over_experts(act, body)

            @block.gpsimd
            def _(pool):
                def split_low(e, i):
                    pool.wait_ge(w_hi, e + 1)
                    pool.tensor_tensor(w1_lo[i][:, :, :], raw1[:, :, :], w1_hi[i][:, :, :].bitcast(F32), ALU.subtract)
                    pool.tensor_tensor(w2_lo[i][:, :, :], raw2[:, :, :], w2_hi[i][:, :, :].bitcast(F32), ALU.subtract)
                    pool.drain().then_inc(w_ready, 1)

                def body(e, i, last):
                    if not moe0:
                        split_low(e, i)
                    for tb in range(NB):
                        for j in range(NU):
                            cols = slice(j * 512, (j + 1) * 512)
                            pool.wait_ge(hf_ready, (e * NB + tb) * NU + j + 1 + U0)
                            pool.tensor_tensor(h_lo[tb % 2][:, cols], hf[:, tb % 2, j, :], h_hi[tb % 2][:, cols].bitcast(F32), ALU.subtract).then_inc(h_ready, 1)
                        if moe0 and tb == 1 and not last:
                            split_low(e + 1, 1 - i)

                if moe0:
                    split_low(0, 0)
                over_experts(pool, body)

            @block.vector
            def _(dve):
                for q, k in ((w_used, R), (y_free, 2), (y_ready, 2), (hf_ready, U0), (w_ready, 1)):
                    dve.sem_inc(q, k)

                def form(e, tb):
                    dve.wait_ge(y_ready, e * NB + tb + 1)
                    dve.wait_ge(sg_ready, e * NB + tb + 1)
                    up = bank[2 * (tb % 2) + 1]
                    dve.tensor_tensor(hf[:, tb % 2, 0, :], sg[:, tb % 2, :], up[:, :], ALU.mult)
                    dve.tensor_tensor(h_hi[tb % 2][:, :], sg[:, tb % 2, :], up[:, :], ALU.mult).then_inc(hf_ready, 1)

                def add(e, tb):
                    dve.wait_ge(y_ready, e * NB + tb + 3)
                    for t in range(TY):
                        tile = tb * TY + t
                        dve.scalar_tensor_tensor(x_res[:, tile, :], y_ps[tb % 2][:, t, :], gate[:, tile, bass.ds(e, 1)], x_res[:, tile, :], ALU.mult, ALU.add)
                    dve.drain().then_inc(y_free, 1)

                def body(e, i, last):
                    for tb in range(NB):
                        if moe0:
                            form(e, tb)
                            if tb >= 1:
                                add(e, tb - 1)
                            elif not (isinstance(e, int) and e == 0):
                                add(e - 1, NB - 1)
                        else:
                            add(e, tb)
                    if last:
                        add(e, NB - 1)

                over_experts(dve, body)


def build(nc, ins, out, stages=STAGES):
    with ExitStack() as ctx:
        x_res = ctx.enter_context(nc.sbuf_tensor("x_res", [P, TILES, D], F32))
        ident = ctx.enter_context(nc.sbuf_tensor("ident", [P, P], F32))
        x_in = nc.alloc_semaphore(name="x_in")
        x_out = nc.alloc_semaphore(name="x_out")
        with nc.Block() as block:
            @block.sync
            def _(sp):
                sp.dma_start(ident[:, :], ins["ident"]).then_inc(x_in, 16)
                sp.dma_start(x_res[:, :, :], ins["x"].rearrange("b (t p) d -> p (b t) d", p=P)).then_inc(x_in, 16)
                sp.wait_ge(x_in, 32)
        phases = ["L0_attn", "L0_xattn", "L0_ffn", "L1_attn", "L1_xattn", "L1_ffn"]
        for name in phases[:stages]:
            part = {k[len(name) + 1:]: v for k, v in ins.items() if k.startswith(name + "_")}
            part.update({k[7:]: v for k, v in ins.items() if k.startswith("shared_")})
            if name in ATTN:
                attention_phase(nc, ATTN[name], x_res, ident, part)
            else:
                expert_phase(nc, name, x_res, ident, part)
        with nc.Block() as block:
            @block.sync
            def _(sp):
                sp.dma_start(out.rearrange("b (t p) d -> p (b t) d", p=P), x_res[:, :, :]).then_inc(x_out, 16)
                sp.wait_ge(x_out, 16)

def layout(inputs):
    import numpy as np

    bf = mybir.dt.np(BF16)
    g = {k: np.asarray(v) for k, v in inputs.items()}
    a = {"ident": np.eye(P, dtype=np.float32), "x": g["x"]}

    def by_rows(wt):
        return wt.reshape(-1, P, wt.shape[1]).transpose(1, 0, 2)

    def column(v):
        return v.reshape(-1, P).T

    zeros = np.zeros(D, np.float32)
    for name, c in ATTN.items():
        w = {k: g.get(f"{name}_{k}") for k in ("Wq", "Wk", "Wv", "Wo", "bq", "bk", "bv", "bo", "Wgk", "bgk", "Wgv", "bgv")}
        for k in ("bq", "bk", "bv", "bo"):
            if w[k] is None:
                w[k] = zeros
        put = {}
        for k in "qkv":
            put["w" + k] = by_rows(w["W" + k].T)
        put["bq"], put["bk"] = column(w["bq"]), column(w["bk"])
        put["bv"], put["bo"] = np.broadcast_to(w["bv"], (P, c.inner)), np.broadcast_to(w["bo"], (P, D))
        wo = np.zeros((c.chunks, c.hpc, c.m, D), np.float32)
        wo[:, :, :c.dk, :] = w["Wo"].T.reshape(c.chunks, c.hpc, c.dk, D)
        put["wo"] = wo.reshape(c.chunks, P, D).transpose(1, 0, 2)
        if c.rope:
            half = c.dk // 2
            swap = np.arange(D).reshape(H, 2, half)[:, ::-1, :].reshape(-1)
            for k in "qk":
                put[f"w{k}r"] = by_rows(w["W" + k][swap].T)
                put[f"b{k}r"] = column(w["b" + k][swap])
            theta = 1.0 / 10000.0 ** (np.arange(0, c.dk, 2, dtype=np.float32) / np.float32(c.dk))
            theta = theta.astype(np.float32)
            ang = np.arange(1, S + 1, dtype=np.float32)[:, None] * theta[None, :]
            ang = np.concatenate([ang, ang], -1)
            sign = np.concatenate([-np.ones(half), np.ones(half)]).astype(np.float32)
            put["cos"] = np.tile(np.cos(ang).astype(np.float32).T, (P // c.dk, 1))
            put["sin"] = np.tile((np.sin(ang).astype(np.float32) * sign).T, (P // c.dk, 1))
        if c.wide:
            put["wgk"], put["wgv"] = by_rows(w["Wgk"].T), by_rows(w["Wgv"].T)
            put["bgk"], put["bgv"] = column(w["bgk"]), np.broadcast_to(w["bgv"], (P, c.inner))
            put["low_ident"] = (np.eye(P) * LOW).astype(bf)
            put["mask"] = g["mask_Bx16xSxS_bk1"]
            put["src"], put["grid"] = g["fside_BxSxS_0"], g["ctx_1024"]
        else:
            put["headmask"] = (np.arange(P)[:, None] // c.dk == np.arange(8)[None, :]).astype(np.float32)
        if c.causal:
            put["ident_bf"] = np.eye(P).astype(bf)
            put["tri"] = np.where(np.arange(P)[:, None] >= np.arange(P)[None, :], 0.0, LOW).astype(bf)
        if c.keymask:
            rest, parts = MASKED, []
            for _ in range(3):
                parts.append(np.asarray(rest).astype(bf))
                rest = rest - float(parts[-1])
            put["masked3"] = np.zeros((P, P), bf)
            put["masked3"][:3] = np.array(parts)[:, None]
            put["mask"] = g["mask_Bx1x1xS2_ik0"].reshape(B, S)
            put["src"] = g["ctx_1024"]
        a.update({f"{name}_{k}": v for k, v in put.items()})
    lower = np.broadcast_to((np.arange(8)[None, :] < np.arange(8)[:, None]).astype(np.float32), (P, 8, 8))
    a.update({
        "L0_ffn_wr": by_rows(g["L0_ffn_w_router"]), "L0_ffn_lower": lower, "L1_ffn_lower": lower,
        "L0_ffn_br": np.broadcast_to(g["L0_ffn_b_router"], (P, 64)),
        "L0_ffn_w_gate": g["L0_ffn_we_gate"], "L0_ffn_w_up": g["L0_ffn_we_up"], "L0_ffn_w_down": g["L0_ffn_we_down"],
        "L0_ffn_ws_gate": g["L0_ffn_ws_gate"], "L0_ffn_ws_up": g["L0_ffn_ws_up"], "L0_ffn_ws_down": g["L0_ffn_ws_down"],
        "L1_ffn_wr": by_rows(g["L1_ffn_gate_w"].T),
        "L1_ffn_w1": g["L1_ffn_w1"].transpose(0, 2, 1), "L1_ffn_w2": g["L1_ffn_w2"].transpose(0, 2, 1),
    })
    return {k: np.ascontiguousarray(v) for k, v in a.items()}

def kernel(**inputs):
    import numpy as np
    import concourse.bacc as bacc
    from concourse.bass_utils import run_bass_kernel_spmd

    nc = bacc.Bacc("TRN2", target_bir_lowering=False, num_devices=1)
    arrays = {f"in_{k}": v for k, v in layout(inputs).items()}
    aps = {k[3:]: nc.dram_tensor(k, v.shape, mybir.dt.from_np(v.dtype), kind="ExternalInput").ap() for k, v in arrays.items()}
    out = nc.dram_tensor("out", (B, S, D), F32, kind="ExternalOutput").ap()
    build(nc, aps, out)
    r = run_bass_kernel_spmd(nc, [arrays], core_ids=[0])
    return r.results[0]["out"]
```

```python
from contextlib import ExitStack

import concourse.bass as bass
from concourse import mybir

F32 = mybir.dt.float32
BF16 = mybir.dt.bfloat16
I32 = mybir.dt.int32
F32R = mybir.dt.float32r
ACT = mybir.ActivationFunctionType
ALU = mybir.AluOpType
AX = mybir.AxisListType

P = 128
B, S, D = 16, 256, 256
H = 16
TT = S // P
DC = D // P
TILES = B * TT
LN_EPS = 1e-5
MASKED = -1e9
LOW = -1e30
STAGES = 6

class Attn:

    def __init__(self, name, dk, keys, causal=False, rope=False, keymask=False, fullmask=False):
        self.name, self.dk, self.keys = name, dk, keys
        self.causal, self.rope, self.keymask, self.fullmask = causal, rope, keymask, fullmask
        self.cross = keymask or fullmask
        self.wide = fullmask
        self.hpc = 1024 // keys
        self.chunks = H // self.hpc
        self.steps = self.chunks * TT
        self.inner = H * dk
        self.groups = self.inner // P
        self.kt = keys // P
        self.m = P // self.hpc
        self.scale = dk ** -0.5

    def key_tiles(self, t):
        return t + 1 if self.causal else self.kt

ATTN = {
    "L0_attn": Attn("L0_attn", 16, S, causal=True),
    "L0_xattn": Attn("L0_xattn", 16, S, keymask=True),
    "L1_attn": Attn("L1_attn", 16, S, causal=True, rope=True),
    "L1_xattn": Attn("L1_xattn", 64, 2 * S, fullmask=True),
}

def tile_pair(x_res, b):
    return x_res[:, bass.ds(b * TT, TT), :]

def attention_phase(nc, c, x_res, ident, ins):
    n = c.name
    with ExitStack() as ctx:
        def sb(name, shape, dt=F32):
            return ctx.enter_context(nc.sbuf_tensor(f"{n}_{name}", shape, dt))

        def sem(name):
            return nc.alloc_semaphore(name=f"{n}_{name}")

        ps = [ctx.enter_context(nc.psum_tensor(f"{n}_bank{i}", [P, 512], F32)) for i in range(4, 8)]
        s_ps = [ctx.enter_context(nc.psum_tensor(f"{n}_scores{i}", [P, c.hpc, c.keys], F32)) for i in range(2)]
        t_ps, a_ps = ps[0:2], ps[2:4]

        wq = sb("wq", [P, DC, c.inner])
        wk = sb("wk", [P, DC, c.inner])
        wv = sb("wv", [P, DC, c.inner])
        wo = sb("wo", [P, c.chunks, D])
        bq = sb("bq", [P, c.groups])
        bk = sb("bk", [P, c.groups])
        bv = sb("bv", [P, c.inner])
        bo = sb("bo", [P, D])
        y_bias = sb("y_bias", [P, TT, D])
        loads = [(wq, "wq"), (wk, "wk"), (wv, "wv"), (wo, "wo"), (bq, "bq"), (bk, "bk"), (bv, "bv"), (bo, "bo")]
        if c.rope:
            wqr = sb("wqr", [P, DC, D])
            wkr = sb("wkr", [P, DC, D])
            bqr = sb("bqr", [P, c.groups])
            bkr = sb("bkr", [P, c.groups])
            cos = sb("cos", [P, S])
            sin = sb("sin", [P, S])
            loads += [(wqr, "wqr"), (wkr, "wkr"), (bqr, "bqr"), (bkr, "bkr"), (cos, "cos"), (sin, "sin")]
        if c.wide:
            wgk = sb("wgk", [P, DC, c.inner])
            wgv = sb("wgv", [P, DC, c.inner])
            bgk = sb("bgk", [P, c.groups])
            bgv = sb("bgv", [P, c.inner])
            loads += [(wgk, "wgk"), (wgv, "wgv"), (bgk, "bgk"), (bgv, "bgv")]
            low_ident = sb("low_ident", [P, P], BF16)
            loads += [(low_ident, "low_ident")]
        else:
            headmask = sb("headmask", [P, 8])
            loads += [(headmask, "headmask")]
        if c.causal:
            ident_bf = sb("ident_bf", [P, P], BF16)
            tri = sb("tri", [P, P], BF16)
            loads += [(ident_bf, "ident_bf"), (tri, "tri")]
        if c.keymask:
            masked3 = sb("masked3", [P, P], BF16)
            loads += [(masked3, "masked3")]

        stats = sb("stats", [P, TT, 6])
        mv = sb("mv", [P, TT, 2])
        rstd = sb("rstd", [P, TT])
        eps_t = sb("eps", [P, TT])
        power = sb("power", [P, TT])
        z = sb("z", [P, TT, D])
        zT = sb("zT", [P, DC, S])
        if c.cross:
            src = sb("src", [P, TT, D])
            srcT = sb("srcT", [P, DC, S])
        else:
            srcT = zT
        if c.wide:
            grid = sb("grid", [P, TT, D])
            gridT = sb("gridT", [P, DC, S])
            qT = sb("qT", [P, H, S])
            kT = sb("kT", [P, c.groups, c.keys])
            v = sb("v", [P, c.kt, H, c.dk])
            mask = sb("mask", [P, 4, c.hpc, S], BF16)
        else:
            qT = sb("qT", [P, c.groups, S])
            kT1 = sb("kT1", [P, c.groups, S])
            kT = sb("kT", [P, H, S])
            v = sb("v", [P, c.kt, H, c.m])
        if c.rope:
            qr = sb("qr", [P, c.groups, S])
            q0 = sb("q0", [P, c.groups, S])
            kr = sb("kr", [P, c.groups, S])
        if c.keymask:
            mask_i = sb("mask_i", [P, S], I32)
            keep = sb("keep", [P, S])
            drop = sb("drop", [P, S], BF16)
        PR = 3
        negmax = sb("negmax", [P, 2, c.hpc])
        lsum = sb("lsum", [P, 2, c.hpc])
        rsum = sb("rsum", [P, 2, c.hpc])
        p = sb("p", [P, PR, c.hpc, c.keys])
        pT = sb("pT", [P, 2, 8, S])
        yT = sb("yT", [P, c.chunks, S])

        loaded = sem("loaded")
        gp_set = sem("gp_set")
        in_loaded = sem("in_loaded")
        in_used = sem("in_used")
        z_ready = sem("z_ready")
        var_ready = sem("var_ready")
        rstd_ready = sem("rstd_ready")
        a_ready = [sem(f"a_ready{i}") for i in range(2)]
        a_free = [sem(f"a_free{i}") for i in range(2)]
        zT_ready = sem("zT_ready")
        kv_ready = sem("kv_ready")
        src_k = sem("src_k")
        src_q = sem("src_q")
        s_ready = sem("s_ready")
        m_ready = sem("m_ready")
        p_ready = sem("p_ready")
        r_ready = sem("r_ready")
        n_ready = sem("n_ready")
        t_ready = sem("t_ready")
        t_done = sem("t_done")
        mask_in = [sem(f"mask_in{i}") for i in range(4)]
        keep_ready = sem("keep_ready")

        NS, NCH = c.steps, c.chunks

        gpu = 2
        uses = (["srcT"] if c.cross else []) + (["gridT"] if c.wide else [])
        if c.wide:
            uses += [f"k{i}" for i in range(c.groups)]
            uses += [f"q{i}" for i in range(c.groups // gpu)]
            uses += [f"v{i}" for i in range(2 * c.kt)]
        else:
            uses += ["k"] + (["kr"] if c.rope else []) + ["q0"] + (["qr"] if c.rope else []) + ["v"]
        if (len(uses) + NCH + 2) % 2:
            uses.append("pad")
        prologue = list(uses)
        uses += ["o0", "o1", "zT"] + [f"o{i}" for i in range(2, NCH)] + ["out"]
        AHEAD = (1, 0)
        UA = len(uses) // 2
        at = {u: i for i, u in enumerate(uses)}

        def bank_wait_free(pe, b, use):
            i = at[use]
            pe.wait_ge(a_free[i % 2], b * UA + i // 2 + 1 + AHEAD[i % 2])
            return a_ps[i % 2], a_ready[i % 2]

        def bank_wait_ready(eng, b, use):
            i = at[use]
            eng.wait_ge(a_ready[i % 2], b * UA + i // 2 + 1 + AHEAD[i % 2])
            return a_ps[i % 2], a_free[i % 2]

        with nc.Block() as block:

            @block.sync
            def _(sp):
                for dst, key in loads:
                    sp.dma_start(dst[:], ins[key]).then_inc(loaded, 16)
                if c.cross:
                    with sp.Fori(0, B, 1) as b:
                        sp.wait_ge(in_used, b * 1 + 1)
                        sp.dma_start(src[:, :, :], ins["src"][bass.ds(b, 1), :, :].rearrange("b (t p) d -> p (b t) d", p=P)).then_inc(in_loaded, 16)
                        if c.wide:
                            sp.dma_start(grid[:, :, :], ins["grid"][bass.ds(b, 1), :, :].rearrange("b (t p) d -> p (b t) d", p=P)).then_inc(in_loaded, 16)
                        if c.keymask:
                            sp.dma_start(mask_i[:, :], ins["mask"][bass.ds(b, 1), :].partition_broadcast(P).rearrange("p b k -> p (b k)")).then_inc(in_loaded, 16)

            @block.gpsimd
            def _(pool):
                pool.memset(eps_t[:, :], LN_EPS).then_inc(gp_set, 1)
                pool.memset(power[:, :], -0.5).then_inc(gp_set, 1)
                if c.wide:
                    pool.memset(qT[:, :, :], 0.0).then_inc(gp_set, 1)
                else:
                    pool.memset(v[:, :, :, :], 0.0).then_inc(gp_set, 1)
                pool.wait_ge(gp_set, 3)
                pool.wait_ge(loaded, 16 * len(loads))
                def inverse_deviation(n_done):
                    pool.wait_ge(var_ready, n_done + 1)
                    pool.tensor_tensor(mv[:, :, 1], mv[:, :, 1], eps_t[:, :], ALU.add)
                    pool.drain()
                    pool.tensor_tensor(rstd[:, :], mv[:, :, 1], power[:, :], ALU.pow).then_inc(rstd_ready, 1)

                inverse_deviation(0)
                with pool.Fori(0, B, 1) as b:
                    if c.wide:
                        def load_mask(s):
                            ch, t = s // TT, s % TT
                            pool.dma_start(mask[:, s % 4, :, :], ins["mask"][bass.ds(b, 1), ch * c.hpc:(ch + 1) * c.hpc, t * P:(t + 1) * P, :].rearrange("b h p k -> p (b h) k")).then_inc(mask_in[s % 4], 16)
                        pool.wait_ge(s_ready, b * NS + 1)
                        for s in range(4):
                            load_mask(s)
                    if not c.wide:
                        if c.rope:
                            for i, (a, r) in enumerate(((kT1, kr), (q0, qr))):
                                pool.wait_ge(src_q if i else src_k, b * 2 + 2)
                                pool.tensor_tensor(a[:, :, :], a[:, :, :], cos[:, None, :].to_broadcast([P, c.groups, S]), ALU.mult)
                                pool.tensor_tensor(r[:, :, :], r[:, :, :], sin[:, None, :].to_broadcast([P, c.groups, S]), ALU.mult)
                                pool.drain()
                                pool.tensor_tensor(qT[:, :, :] if i else a[:, :, :], a[:, :, :], r[:, :, :], ALU.add)
                            pool.drain()
                        else:
                            pool.wait_ge(src_k, b + 1)
                        for ch in range(NCH):
                            heads = slice((ch % 2) * 4, (ch % 2) * 4 + 4)
                            pool.tensor_tensor(kT[:, 4 * ch:4 * ch + 4, :], kT1[:, ch // 2:ch // 2 + 1, :].to_broadcast([P, 4, S]),
                                               headmask[:, heads, None].to_broadcast([P, 4, S]), ALU.mult).then_inc(kv_ready, 1)
                    for s in range(NS):
                        t = s % TT
                        nk = P * c.key_tiles(t)
                        if c.wide and s >= 1 and s + 3 < NS:
                            pool.wait_ge(s_ready, b * NS + s + 1)
                            load_mask(s + 3)
                        pool.wait_ge(r_ready, b * NS + s + 1)
                        pool.tensor_tensor(p[:, s % PR, :, 0:nk], p[:, s % PR, :, 0:nk],
                                           rsum[:, s % 2, :, None].to_broadcast([P, c.hpc, nk]), ALU.mult).then_inc(n_ready, 1)
                        if s == 2:
                            inverse_deviation(b + 1)

            @block.vector
            def _(dve):
                for k in range(2):
                    dve.sem_inc(a_free[k], 1)
                if c.wide:
                    dve.sem_inc(s_ready, 1)
                if c.cross:
                    dve.sem_inc(in_used, 1)
                dve.wait_ge(loaded, 16 * len(loads))
                dve.wait_ge(gp_set, 3)

                def statistics(seq):
                    for t in range(TT):
                        dve.bn_stats(stats[:, t, :], x_res[:, bass.ds(seq * TT + t, 1), :])
                    dve.drain()
                    for t in range(TT):
                        e = dve.bn_aggr(mv[:, t, :], stats[:, t, :])
                    e.then_inc(var_ready, 1)

                def normalise(seq):
                    dve.drain()
                    dve.wait_ge(rstd_ready, seq + 1)
                    for t in range(TT):
                        e = dve.tensor_scalar(z[:, t, :], x_res[:, bass.ds(seq * TT + t, 1), :], mv[:, t, 0:1], rstd[:, t:t + 1], ALU.subtract, ALU.mult)
                    e.then_inc(z_ready, 1)

                statistics(0)
                normalise(0)
                with dve.Fori(0, B, 1) as b:
                    if c.keymask:
                        dve.wait_ge(in_loaded, b * 32 + 32)
                        dve.tensor_scalar(keep[:, :], mask_i[:, :], 0, None, ALU.not_equal)
                        dve.tensor_scalar(drop[:, :], mask_i[:, :], 0, None, ALU.is_equal).then_inc(keep_ready, 1)
                    if c.keymask:
                        dve.drain()
                        bank, free = bank_wait_ready(dve, b, "k")
                        for g in range(c.groups):
                            e = dve.scalar_tensor_tensor(kT1[:, g, :], bank[:, g * S:(g + 1) * S], bk[:, g:g + 1], keep[:, :], ALU.add, ALU.mult)
                        e.then_inc(free, 1)
                        dve.drain().then_inc(src_k, 1)

                    for i in range(c.groups // gpu):
                        bank, free = bank_wait_ready(dve, b, f"q{i}")
                        for j in range(gpu):
                            g = i * gpu + j
                            if c.wide:
                                for r in range(2):
                                    rows = slice(64 * r, 64 * r + 64)
                                    e = dve.tensor_scalar(qT[rows, 2 * g + r, :], bank[rows, j * S:(j + 1) * S], bq[rows, g:g + 1], c.scale, ALU.add, ALU.mult)
                            else:
                                e = dve.tensor_scalar((q0 if c.rope else qT)[:, g, :], bank[:, j * S:(j + 1) * S], bq[:, g:g + 1], c.scale, ALU.add, ALU.mult)
                        e.then_inc(free, 1)
                        if c.rope:
                            dve.drain().then_inc(src_q, 1)
                            bank, free = bank_wait_ready(dve, b, "qr")
                            for g in range(c.groups):
                                e = dve.tensor_scalar(qr[:, g, :], bank[:, g * S:(g + 1) * S], bqr[:, g:g + 1], c.scale, ALU.add, ALU.mult)
                            e.then_inc(free, 1)
                            dve.drain().then_inc(src_q, 1)
                    for u in prologue:
                        if u[0] != "v":
                            continue
                        bank, free = bank_wait_ready(dve, b, u)
                        if c.wide:
                            i = int(u[1:])
                            cols = slice((i % 2) * 512, (i % 2) * 512 + 512)
                            bias = (bv if i // 2 < TT else bgv)[:, cols]
                            e = dve.tensor_tensor(v[:, i // 2, 8 * (i % 2):8 * (i % 2) + 8, :], bank[:, :].rearrange("p (h d) -> p h d", d=c.dk),
                                                  bias.rearrange("p (h d) -> p h d", d=c.dk), ALU.add)
                        else:
                            for t in range(TT):
                                e = dve.tensor_tensor(v[:, t, :, 0:c.dk], bank[:, t * D:(t + 1) * D].rearrange("p (h d) -> p h d", d=c.dk),
                                                      bv[:, :].rearrange("p (h d) -> p h d", d=c.dk), ALU.add)
                        e.then_inc(free, 1)

                    def row_max(s):
                        t = s % TT
                        nk = P * c.key_tiles(t)
                        dve.wait_ge(s_ready, b * NS + s + 1 + int(c.wide))
                        dve.tensor_reduce(negmax[:, s % 2, :], s_ps[s % 2][:, :, 0:nk], AX.X, ALU.max, negate=True).then_inc(m_ready, 1)

                    def copy_flipped(s):
                        ch, t = s // TT, s % TT
                        for hh in range(2):
                            dve.wait_ge(t_ready, (b * NS + s) * 2 + hh + 1)
                            dst = pT[:, ch % 2, 4 * hh:4 * hh + 4, t * P:(t + 1) * P]
                            view = t_ps[hh][:, :].rearrange("p (a q) -> p a q", q=P)
                            if c.key_tiles(t) == 1:
                                dst = pT[:, ch % 2, 4 * hh:4 * hh + 3:2, t * P:(t + 1) * P]
                                view = view[:, 0:3:2, :]
                            dve.tensor_copy(dst, view).then_inc(t_done, 1)

                    row_max(0)
                    if c.cross:
                        dve.drain().then_inc(in_used, 1)
                    row_max(1)
                    for s in range(NS):
                        dve.wait_ge(p_ready, b * NS + s + 1)
                        dve.reciprocal(rsum[:, s % 2, :], lsum[:, s % 2, :]).then_inc(r_ready, 1)
                        if s + 2 < NS:
                            row_max(s + 2)
                        if s >= 1:
                            copy_flipped(s - 1)
                        if s == 1:
                            statistics(b + 1)
                        if s == 3:
                            normalise(b + 1)
                    copy_flipped(NS - 1)
                    bank, free = bank_wait_ready(dve, b, "out")
                    dve.tensor_tensor(y_bias[:, :, :], bank[:, :].rearrange("p (t d) -> p t d", d=D), bo[:, None, :].to_broadcast([P, TT, D]), ALU.add).then_inc(free, 1)
                    dve.drain()
                    dve.tensor_tensor(tile_pair(x_res, b), y_bias[:, :, :], tile_pair(x_res, b), ALU.add)
                    dve.drain()

            @block.scalar
            def _(act):
                act.wait_ge(loaded, 16 * len(loads))
                act.wait_ge(gp_set, 3)
                act.wait_ge(a_ready[0], 1)
                act.activation(zT[:, :, :], a_ps[0][:, :].rearrange("p (c q) -> p c q", q=S), ACT.Copy).then_inc(a_free[0], 1)
                act.drain().then_inc(zT_ready, 1)
                with act.Fori(0, B, 1) as b:
                    def copy_out(use, pieces):
                        bank, free = bank_wait_ready(act, b, use)
                        for dst, src_ap, bias in pieces(bank):
                            if bias is None:
                                e = act.activation(dst, src_ap, ACT.Copy)
                            else:
                                e = act.activation(dst, src_ap, ACT.Identity, bias=bias)
                        e.then_inc(free, 1)
                        return e

                    def half(bank, j):
                        return bank[:, j * S:(j + 1) * S]

                    for u in prologue:
                        if u in ("srcT", "gridT"):
                            dst = srcT if u == "srcT" else gridT
                            copy_out(u, lambda bank: [(dst[:, :, :], bank[:, :].rearrange("p (c q) -> p c q", q=S), None)])
                        elif u == "k" and not c.keymask:
                            copy_out(u, lambda bank: [(kT1[:, g, :], half(bank, g), bk[:, g:g + 1]) for g in range(c.groups)])
                            act.drain().then_inc(src_k, 1)
                        elif u == "kr":
                            copy_out(u, lambda bank: [(kr[:, g, :], half(bank, g), bkr[:, g:g + 1]) for g in range(c.groups)])
                            act.drain().then_inc(src_k, 1)
                        elif u == "pad":
                            copy_out(u, lambda bank: [(yT[0:1, 0, 0:1], bank[0:1, 0:1], None)])
                        elif c.wide and u[0] == "k":
                            g = int(u[1:])
                            copy_out(u, lambda bank: [(kT[:, g, 0:S], half(bank, 0), bk[:, g:g + 1]), (kT[:, g, S:2 * S], half(bank, 1), bgk[:, g:g + 1])])
                    def copy_output(ch):
                        copy_out(f"o{ch}", lambda bank: [(yT[:, ch, :], half(bank, 0), None)])

                    for s in range(NS):
                        t = s % TT
                        nk = P * c.key_tiles(t)
                        act.wait_ge(m_ready, b * NS + s + 1)
                        if s >= PR:
                            act.wait_ge(t_ready, (b * NS + s - PR + 1) * 2)
                        for i in range(c.hpc):
                            e = act.activation(p[:, s % PR, i, 0:nk], s_ps[s % 2][:, i, 0:nk], ACT.Exp, bias=negmax[:, s % 2, i:i + 1], accum_out=lsum[:, s % 2, i:i + 1])
                        e.then_inc(p_ready, 1)
                        if s >= 5 and s % TT == 1:
                            copy_output((s - 5) // TT)
                        if s == 7:
                            copy_out("zT", lambda bank: [(zT[:, :, :], bank[:, :].rearrange("p (c q) -> p c q", q=S), None)])
                            act.drain().then_inc(zT_ready, 1)
                    for ch in range((NS - 6) // TT + 1, NCH):
                        copy_output(ch)

            @block.tensor
            def _(pe):
                pe.wait_ge(loaded, 16 * len(loads))
                pe.wait_ge(gp_set, 3)
                def transpose_tiles(bank, ready, tiles):
                    for cc in range(DC):
                        for t in range(TT):
                            e = pe.transpose(bank[:, cc * S + t * P:cc * S + (t + 1) * P], tiles[:, t, cc * P:(cc + 1) * P], ident[:, :])
                    e.then_inc(ready, 1)

                pe.wait_ge(z_ready, 1)
                pe.wait_ge(a_free[0], 1)
                transpose_tiles(a_ps[0], a_ready[0], z)
                with pe.Fori(0, B, 1) as b:
                    def transposes(use, tiles):
                        bank, ready = bank_wait_free(pe, b, use)
                        transpose_tiles(bank, ready, tiles)

                    def project(out, w, g, xT):
                        for cc in range(DC):
                            e = pe.matmul(out, w[:, cc, g * P:(g + 1) * P], xT[:, cc, :], start=cc == 0, stop=cc == DC - 1)
                        return e

                    def project_rows(out, xT, t, w, c0, cols):
                        for cc in range(DC):
                            e = pe.matmul(out, xT[:, cc, t * P:(t + 1) * P], w[:, cc, c0:c0 + cols], start=cc == 0, stop=cc == DC - 1)
                        return e

                    for u in prologue:
                        if u == "srcT":
                            per = 16 * (1 + int(c.wide) + int(c.keymask))
                            pe.wait_ge(in_loaded, b * per + per)
                            transposes("srcT", src)
                        elif u == "gridT":
                            transposes("gridT", grid)
                        elif u == "pad":
                            bank, ready = bank_wait_free(pe, b, u)
                            pe.matmul(bank[:, 0:P], ident[:, :], ident[:, :], start=True, stop=True).then_inc(ready, 1)
                        else:
                            if u in ("k", "k0"):
                                pe.wait_ge(zT_ready, b + 1)
                                for last in ("srcT", "gridT")[:int(c.cross) + int(c.wide)]:
                                    pe.wait_ge(a_free[at[last] % 2], b * UA + at[last] // 2 + 2 + AHEAD[at[last] % 2])
                            bank, ready = bank_wait_free(pe, b, u)
                            if u[0] == "q":
                                w = wqr if u == "qr" else wq
                                i = 0 if u == "qr" else int(u[1:])
                                for j in range(gpu):
                                    e = project(bank[:, j * S:(j + 1) * S], w, i * gpu + j, zT)
                            elif u in ("k", "kr"):
                                for g in range(c.groups):
                                    e = project(bank[:, g * S:(g + 1) * S], wk if u == "k" else wkr, g, srcT)
                            elif u == "v":
                                for t in range(TT):
                                    e = project_rows(bank[:, t * D:(t + 1) * D], srcT, t, wv, 0, D)
                            elif u[0] == "k":
                                g = int(u[1:])
                                project(bank[:, 0:S], wk, g, srcT)
                                e = project(bank[:, S:2 * S], wgk, g, gridT)
                            else:
                                i = int(u[1:])
                                kt, cols = i // 2, 512
                                own = kt < TT
                                e = project_rows(bank[:, :], srcT if own else gridT, kt % TT, wv if own else wgv, (i % 2) * cols, cols)
                            e.then_inc(ready, 1)
                    def copied(u):
                        pe.wait_ge(a_free[at[u] % 2], b * UA + at[u] // 2 + 2 + AHEAD[at[u] % 2])

                    if not c.rope:
                        copied(f"q{c.groups // gpu - 1}")
                    if c.keymask:
                        pe.wait_ge(keep_ready, b + 1)

                    def scores(s):
                        ch, t = s // TT, s % TT
                        nk = P * c.key_tiles(t)
                        out = s_ps[s % 2]
                        if s >= 2:
                            pe.wait_ge(p_ready, b * NS + s - 1)
                        q0_, q1_ = t * P, (t + 1) * P
                        if c.wide:
                            pe.wait_ge(mask_in[s % 4], (b * (NS // 4) + s // 4) * 16 + 16)
                            for i in range(c.hpc):
                                pe.matmul(out[:, i, :], qT[:, ch * c.hpc + i, q0_:q1_], kT[:, ch, :], start=True, stop=False, skip_group_check=True)
                                e = pe.matmul(out[:, i, 0:S], low_ident[:, :], mask[:, s % 4, i, :], start=False, stop=True, skip_group_check=True)
                        else:
                            g = ch // 2
                            if t == 0:
                                pe.wait_ge(kv_ready, b * NCH + ch + 1)
                            for hh in range(2):
                                h0 = ch * 4 + hh * 2
                                o = out[:, 2 * hh:2 * hh + 2, 0:nk]
                                e = pe.matmul(o, qT[:, g, q0_:q1_], kT[:, h0:h0 + 2, 0:nk], start=True, stop=not (c.causal or c.keymask), skip_group_check=True)
                                if c.causal:
                                    e = pe.matmul(out[:, 2 * hh:2 * hh + 2, q0_:q1_], ident_bf[:, :], tri[:, None, :].to_broadcast([P, 2, P]), start=False, stop=True, skip_group_check=True)
                                if c.keymask:
                                    e = pe.matmul(o, masked3[:, :], drop[:, None, :].to_broadcast([P, 2, S]), start=False, stop=True, skip_group_check=True)
                        e.then_inc(s_ready, 1)

                    def flip(s):
                        t = s % TT
                        pe.wait_ge(n_ready, b * NS + s + 1)
                        heads = c.hpc // 2
                        for hh in range(2):
                            if s >= 1:
                                pe.wait_ge(t_done, (b * NS + s - 1) * 2 + hh + 1)
                            for i in range(heads):
                                for k in range(c.key_tiles(t)):
                                    col = (i * c.kt + k) * P
                                    e = pe.transpose(t_ps[hh][:, col:col + P], p[:, s % PR, hh * heads + i, k * P:(k + 1) * P], ident[:, :])
                            e.then_inc(t_ready, 1)

                    def values(ch):
                        if ch == 0:
                            for u in prologue[-2:]:
                                copied(u)
                        pe.wait_ge(t_done, (b * NS + ch * TT + TT) * 2)
                        bank, ready = bank_wait_free(pe, b, f"o{ch}")
                        for i in range(c.hpc):
                            for k in range(c.kt):
                                q0_ = k * P if c.causal else 0
                                e = pe.matmul(bank[i * c.m:(i + 1) * c.m, q0_:S], v[:, k, ch * c.hpc + i, :], pT[:, ch % 2, i * c.kt + k, q0_:S],
                                              start=k == 0, stop=k == c.kt - 1, skip_group_check=True)
                        e.then_inc(ready, 1)

                    scores(0)
                    scores(1)
                    for s in range(NS + 1):
                        if s + 2 < NS:
                            scores(s + 2)
                        if s >= 1:
                            flip(s - 1)
                        if s >= 3 and s % TT == 1:
                            values((s - 3) // TT)
                        if s == 6:
                            pe.wait_ge(z_ready, b + 2)
                            transposes("zT", z)
                    values(NCH - 1)
                    for u in (f"o{NCH - 2}", f"o{NCH - 1}"):
                        pe.wait_ge(a_free[at[u] % 2], b * UA + at[u] // 2 + 2 + AHEAD[at[u] % 2])
                    bank, ready = bank_wait_free(pe, b, "out")
                    for t in range(TT):
                        o = bank[:, t * D:(t + 1) * D]
                        for ch in range(NCH):
                            e = pe.matmul(o, yT[:, ch, t * P:(t + 1) * P], wo[:, ch, :], start=ch == 0, stop=ch == NCH - 1)
                    e.then_inc(ready, 1)

def expert_phase(nc, layer, x_res, ident, ins):
    moe0 = layer == "L0_ffn"
    n = layer
    E = 64 if moe0 else 8
    F = P if moe0 else 1024
    NF = F // P
    SH = 1 if moe0 else 0
    TB = 512 if moe0 else 256
    NB = B * S // TB
    with ExitStack() as ctx:
        def sb(name, shape, dt=F32):
            return ctx.enter_context(nc.sbuf_tensor(f"{n}_{name}", shape, dt))

        def sem(name):
            return nc.alloc_semaphore(name=f"{n}_{name}")

        bank = [ctx.enter_context(nc.psum_tensor(f"{n}_bank{i}", [P, 512], F32)) for i in range(4)]
        y_ps = [ctx.enter_context(nc.psum_tensor(f"{n}_y{i}", [P, TB // P, D], F32)) for i in range(2)]
        z_hi = sb("z_hi", [P, DC, B * S], F32R)
        z_lo = sb("z_lo", [P, DC, B * S], F32R)
        gate = sb("gate", [P, TILES, SH + E])

        with ExitStack() as rctx:
            def rb(name, shape, dt=F32):
                return rctx.enter_context(nc.sbuf_tensor(f"{n}_{name}", shape, dt))
            wr = rb("wr", [P, DC, E])
            stats = rb("stats", [P, TT, 6])
            mv = rb("mv", [P, TT, 2])
            rstd = rb("rstd", [P, TT])
            eps_t = rb("eps", [P, TT])
            power = rb("power", [P, TT])
            z = rb("z", [P, TT, D])
            zT = rb("zT", [P, DC, S])
            sc = rb("sc", [P, TT, E])
            swb = rb("swb", [P, TT, E])
            br = rb("br", [P, E])
            lower = rb("lower", [P, 8, 8])
            top = rb("top", [P, TT, 8, 8])
            gs = rb("gs", [P, TT, 8])
            cmp = rb("cmp", [P, TT, 8, 8])
            eq = rb("eq", [P, TT, 8, 8])
            rank = rb("rank", [P, TT, 8])
            msk = rb("msk", [P, TT, E])
            top8 = rb("top8", [P, TT, 8])
            sel = rb("sel", [P, TT, E])
            wsum = rb("wsum", [P, TT])
            loaded = sem("r_loaded")
            gp_set = sem("r_gp_set")
            var_ready = sem("r_var_ready")
            rstd_ready = sem("r_rstd_ready")
            z_ready = sem("r_z_ready")
            t_ready = sem("r_t_ready")
            t_act = sem("r_t_act")
            t_dve = sem("r_t_dve")
            l_ready = sem("r_l_ready")
            sc_ready = sem("r_sc_ready")
            sc_used = sem("r_sc_used")
            rloads = [(wr, "wr"), (lower, "lower")] + ([(br, "br")] if moe0 else [])
            with nc.Block() as block:
                @block.sync
                def _(sp):
                    for dst, key in rloads:
                        sp.dma_start(dst[:], ins[key]).then_inc(loaded, 16)

                @block.gpsimd
                def _(pool):
                    pool.memset(eps_t[:, :], LN_EPS).then_inc(gp_set, 1)
                    pool.memset(power[:, :], -0.5).then_inc(gp_set, 1)
                    pool.wait_ge(gp_set, 2)
                    with pool.Fori(0, B + 1, 1) as b:
                        pool.wait_ge(var_ready, b + 1)
                        pool.tensor_tensor(mv[:, :, 1], mv[:, :, 1], eps_t[:, :], ALU.add)
                        pool.drain()
                        pool.tensor_tensor(rstd[:, :], mv[:, :, 1], power[:, :], ALU.pow).then_inc(rstd_ready, 1)

                @block.vector
                def _(dve):
                    dve.sem_inc(t_act, 1)
                    dve.sem_inc(t_dve, 1)
                    dve.sem_inc(sc_used, 1)
                    if SH:
                        dve.memset(gate[:, :, 0:1], 1.0)
                    dve.wait_ge(loaded, 16 * len(rloads))

                    def normalise(seq):
                        for t in range(TT):
                            dve.bn_stats(stats[:, t, :], x_res[:, bass.ds(seq * TT + t, 1), :])
                        dve.drain()
                        for t in range(TT):
                            e = dve.bn_aggr(mv[:, t, :], stats[:, t, :])
                        e.then_inc(var_ready, 1)
                        dve.drain()
                        dve.wait_ge(rstd_ready, seq + 1)
                        for t in range(TT):
                            e = dve.tensor_scalar(z[:, t, :], x_res[:, bass.ds(seq * TT + t, 1), :], mv[:, t, 0:1], rstd[:, t:t + 1], ALU.subtract, ALU.mult)
                        e.then_inc(z_ready, 1)

                    def count_better(values):
                        shape = [P, TT, 8, 8]
                        other, own = values[:, :, None, :].to_broadcast(shape), values[:, :, :, None].to_broadcast(shape)
                        dve.tensor_tensor(cmp[:, :, :, :], other, own, ALU.is_gt)
                        dve.tensor_tensor(eq[:, :, :, :], other, own, ALU.is_equal)
                        dve.drain()
                        dve.tensor_tensor(eq[:, :, :, :], eq[:, :, :, :], lower[:, None, :, :].to_broadcast(shape), ALU.mult)
                        dve.drain()
                        dve.tensor_tensor(cmp[:, :, :, :], cmp[:, :, :, :], eq[:, :, :, :], ALU.add)
                        dve.drain()
                        dve.tensor_reduce(rank[:, :, :], cmp[:, :, :, :], AX.X, ALU.add)
                        dve.drain()

                    normalise(0)
                    with dve.Fori(0, B, 1) as b:
                        dve.wait_ge(t_act, b + 2)
                        dve.tensor_copy(z_hi[:, :, bass.ds(b * S, S)], zT[:, :, :])
                        dve.drain()
                        dve.tensor_tensor(z_lo[:, :, bass.ds(b * S, S)], zT[:, :, :], z_hi[:, :, bass.ds(b * S, S)].bitcast(F32), ALU.subtract).then_inc(t_dve, 1)
                        normalise(b + 1)
                        gates = gate[:, bass.ds(b * TT, TT), SH:]
                        dve.wait_ge(sc_ready, b + 1)
                        if moe0:
                            dve.tensor_tensor(swb[:, :, :], sc[:, :, :], br[:, None, :].to_broadcast([P, TT, E]), ALU.add)
                            dve.drain()
                            for t in range(TT):
                                for g in range(8):
                                    dve.max(top[:, t, g, :], swb[:, t, 8 * g:8 * g + 8])
                            dve.drain()
                            dve.tensor_tensor(gs[:, :, :], top[:, :, :, 0], top[:, :, :, 1], ALU.add)
                            dve.drain()
                            count_better(gs)
                            dve.tensor_scalar(rank[:, :, :], rank[:, :, :], 4.0, None, ALU.is_lt)
                            dve.drain()
                            dve.tensor_tensor(msk[:, :, :].rearrange("p t (g e) -> p (t g) e", e=8), swb[:, :, :].rearrange("p t (g e) -> p (t g) e", e=8),
                                              rank[:, :, :].rearrange("p t g -> p (t g)")[:, :, None].to_broadcast([P, TT * 8, 8]), ALU.mult)
                            dve.drain()
                            for t in range(TT):
                                dve.max(top8[:, t, :], msk[:, t, :])
                            dve.drain()
                            for t in range(TT):
                                dve.match_replace(sel[:, t, :], top8[:, t, :], msk[:, t, :], -1e30)
                            dve.drain()
                            dve.scalar_tensor_tensor(sel[:, :, :], sel[:, :, :], -1e29, sc[:, :, :], ALU.is_lt, ALU.mult)
                            dve.drain()
                            dve.tensor_reduce(wsum[:, :], sel[:, :, :], AX.X, ALU.add)
                            dve.drain()
                            dve.tensor_scalar(wsum[:, :], wsum[:, :], 1e-20, None, ALU.add)
                            dve.drain()
                            dve.reciprocal(wsum[:, :], wsum[:, :])
                            dve.drain()
                            dve.scalar_tensor_tensor(gates, sel[:, :, :], 2.5, wsum[:, :, None].to_broadcast([P, TT, E]), ALU.mult, ALU.mult)
                        else:
                            dve.tensor_reduce(wsum[:, :], sc[:, :, :], AX.X, ALU.max)
                            count_better(sc)
                            dve.tensor_scalar(rank[:, :, :], rank[:, :, :], 2.0, LOW, ALU.is_ge, ALU.mult)
                            dve.tensor_tensor(sel[:, :, :], sc[:, :, :], wsum[:, :, None].to_broadcast([P, TT, E]), ALU.subtract)
                            dve.drain()
                            dve.tensor_tensor(gates, sel[:, :, :], rank[:, :, :], ALU.add)
                        dve.drain().then_inc(sc_used, 1)

                @block.scalar
                def _(act):
                    with act.Fori(0, B, 1) as b:
                        act.wait_ge(t_ready, b + 1)
                        act.activation(zT[:, :, :], bank[0][:, :].rearrange("p (c q) -> p c q", q=S), ACT.Copy).then_inc(t_act, 1)
                        act.wait_ge(sc_used, b + 1)
                        act.wait_ge(l_ready, b + 1)
                        act.activation(sc[:, :, :], bank[1][:, 0:TT * E].rearrange("p (t e) -> p t e", e=E), ACT.Sigmoid if moe0 else ACT.Copy).then_inc(sc_ready, 1)

                @block.tensor
                def _(pe):
                    pe.wait_ge(loaded, 16 * len(rloads))
                    with pe.Fori(0, B, 1) as b:
                        pe.wait_ge(z_ready, b + 1)
                        pe.wait_ge(t_act, b + 1)
                        pe.wait_ge(t_dve, b + 1)
                        for cc in range(DC):
                            for t in range(TT):
                                e = pe.transpose(bank[0][:, cc * S + t * P:cc * S + (t + 1) * P], z[:, t, cc * P:(cc + 1) * P], ident[:, :])
                        e.then_inc(t_ready, 1)
                        pe.wait_ge(t_act, b + 2)
                        pe.wait_ge(sc_used, b + 1)
                        for t in range(TT):
                            for cc in range(DC):
                                e = pe.matmul(bank[1][:, t * E:(t + 1) * E], zT[:, cc, t * P:(t + 1) * P], wr[:, cc, :], start=cc == 0, stop=cc == DC - 1)
                        e.then_inc(l_ready, 1)

            if not moe0:
                e_done = sem("r_e_done")
                gsum = rb("gsum", [P, TILES])
                with nc.Block() as block:
                    @block.scalar
                    def _(act):
                        act.activation(gate[:, :, :], gate[:, :, :], ACT.Exp).then_inc(e_done, 1)

                    @block.vector
                    def _(dve):
                        dve.wait_ge(e_done, 1)
                        dve.tensor_reduce(gsum[:, :], gate[:, :, :], AX.X, ALU.add)
                        dve.drain()
                        dve.reciprocal(gsum[:, :], gsum[:, :])
                        dve.drain()
                        dve.tensor_tensor(gate[:, :, :], gate[:, :, :], gsum[:, :, None].to_broadcast([P, TILES, E]), ALU.mult)

        R = 2 if moe0 else 1
        W1 = 2 * F if moe0 else F
        NU = 1 if moe0 else F * TB // (P * 512)
        TY = TB // P
        LAST = SH + E - 1
        raw1 = sb("raw1", [P, DC, W1])
        raw2 = sb("raw2", [P, NF, D])
        w1_hi = [sb(f"w1_hi{i}", [P, DC, W1], F32R) for i in range(R)]
        w1_lo = [sb(f"w1_lo{i}", [P, DC, W1], F32R) for i in range(R)]
        w2_hi = [sb(f"w2_hi{i}", [P, NF, D], F32R) for i in range(R)]
        w2_lo = [sb(f"w2_lo{i}", [P, NF, D], F32R) for i in range(R)]
        hf = sb("hf", [P, 2, NU, 512])
        h_hi = [sb(f"h_hi{i}", [P, NU * 512], F32R) for i in range(2)]
        h_lo = [sb(f"h_lo{i}", [P, NU * 512], F32R) for i in range(2)]
        sg = sb("sg", [P, 2, 512]) if moe0 else None
        w_in = sem("w_in")
        w_hi = sem("w_hi")
        w_ready = sem("w_ready")
        w_used = sem("w_used")
        h_ps = sem("h_ps")
        sg_ready = sem("sg_ready")
        U0 = 2 if moe0 else 4
        hf_ready = sem("hf_ready")
        h_ready = sem("h_ready")
        y_ready = sem("y_ready")
        y_free = sem("y_free")
        WD = 16 * (3 if moe0 else 2)

        with nc.Block() as block:

            @block.sync
            def _(sp):
                if SH:
                    sp.wait_ge(w_ready, 1)
                    sp.dma_start(raw1[:, :, 0:F], ins["ws_gate"].rearrange("(c p) f -> p c f", p=P)).then_inc(w_in, 16)
                    sp.dma_start(raw1[:, :, F:2 * F], ins["ws_up"].rearrange("(c p) f -> p c f", p=P)).then_inc(w_in, 16)
                    sp.dma_start(raw2[:, 0, :], ins["ws_down"]).then_inc(w_in, 16)
                with sp.Fori(0, E, 1) as e:
                    sp.wait_ge(w_ready, e + SH + 1)
                    if moe0:
                        sp.dma_start(raw1[:, :, 0:F], ins["w_gate"][bass.ds(e, 1), :, :].rearrange("e (c p) f -> p (e c) f", p=P)).then_inc(w_in, 16)
                        sp.dma_start(raw1[:, :, F:2 * F], ins["w_up"][bass.ds(e, 1), :, :].rearrange("e (c p) f -> p (e c) f", p=P)).then_inc(w_in, 16)
                        sp.dma_start(raw2[:, :, :], ins["w_down"][bass.ds(e, 1), :, :].rearrange("e p d -> p e d")).then_inc(w_in, 16)
                    else:
                        sp.dma_start(raw1[:, :, :], ins["w1"][bass.ds(e, 1), :, :].rearrange("e (c p) f -> p (e c) f", p=P)).then_inc(w_in, 16)
                        sp.dma_start(raw2[:, :, :], ins["w2"][bass.ds(e, 1), :, :].rearrange("e (f p) d -> p (e f) d", p=P)).then_inc(w_in, 16)

            def over_experts(eng, body):
                if moe0:
                    body(0, 0, False)
                    with eng.Fori(0, E // 2 - 1, 1) as pair:
                        body(pair * 2 + 1, 1, False)
                        body(pair * 2 + 2, 0, False)
                    body(E - 1, 1, False)
                    body(E, 0, True)
                else:
                    with eng.Fori(0, E, 1) as e:
                        body(e, 0, False)

            @block.tensor
            def _(pe):
                def three(out, a_hi, a_lo, b_hi, b_lo, first, last):
                    pe.matmul(out, a_lo, b_hi, start=first, stop=False, skip_group_check=True)
                    pe.matmul(out, a_hi, b_lo, start=False, stop=False, skip_group_check=True)
                    return pe.matmul(out, a_hi, b_hi, start=False, stop=last, skip_group_check=True)

                def hidden(e, i, tb):
                    cols = slice(tb * TB, (tb + 1) * TB)
                    for j in range(NU):
                        pe.wait_ge(hf_ready, (e * NB + tb) * NU + j + 1)
                        for u in range(2):
                            out = bank[2 * (tb % 2) + u][:, :] if moe0 else bank[j][:, u * TB:(u + 1) * TB]
                            rows = slice((2 * j + u) * P, (2 * j + u + 1) * P)
                            for cc in range(DC):
                                m = three(out, w1_hi[i][:, cc, rows], w1_lo[i][:, cc, rows], z_hi[:, cc, cols], z_lo[:, cc, cols], cc == 0, cc == DC - 1)
                        m.then_inc(h_ps, 1)

                def down(e, i, tb):
                    pe.wait_ge(h_ready, (e * NB + tb + 1) * NU)
                    pe.wait_ge(y_free, e * NB + tb + 1)
                    for t in range(TY):
                        for f in range(NF):
                            cols = slice(f * TB + t * P, f * TB + (t + 1) * P)
                            m = three(y_ps[tb % 2][:, t, :], h_hi[tb % 2][:, cols], h_lo[tb % 2][:, cols], w2_hi[i][:, f, :], w2_lo[i][:, f, :], f == 0, f == NF - 1)
                    m.then_inc(y_ready, 1)

                def body(e, i, last):
                    pe.wait_ge(w_ready, e + 2)
                    for tb in range(NB):
                        hidden(e, i, tb)
                        if tb >= 1:
                            down(e, i, tb - 1)
                        elif moe0 and not (isinstance(e, int) and e == 0):
                            down(e - 1, 1 - i, NB - 1)
                            pe.drain().then_inc(w_used, 1)
                    if last or not moe0:
                        down(e, i, NB - 1)
                        pe.drain().then_inc(w_used, 1)

                over_experts(pe, body)

            @block.scalar
            def _(act):
                def split_high(e, i):
                    act.wait_ge(w_in, e * WD + WD)
                    act.wait_ge(w_used, e + 1)
                    act.activation(w1_hi[i][:, :, :], raw1[:, :, :], ACT.Copy)
                    act.activation(w2_hi[i][:, :, :], raw2[:, :, :], ACT.Copy).then_inc(w_hi, 1)

                def body(e, i, last):
                    if not moe0:
                        split_high(e, i)
                    for tb in range(NB):
                        if moe0:
                            act.wait_ge(h_ps, e * NB + tb + 1)
                            act.wait_ge(hf_ready, e * NB + tb + 1)
                            act.activation(sg[:, tb % 2, :], bank[2 * (tb % 2)][:, :], ACT.Silu).then_inc(sg_ready, 1)
                            if tb == 1 and not last:
                                split_high(e + 1, 1 - i)
                        else:
                            act.wait_ge(y_ready, e * NB + tb + 1)
                            for j in range(NU):
                                act.wait_ge(h_ps, (e * NB + tb) * NU + j + 1)
                                act.activation(hf[:, tb % 2, j, :], bank[j][:, :], ACT.Relu)
                                act.activation(h_hi[tb % 2][:, j * 512:(j + 1) * 512], bank[j][:, :], ACT.Relu).then_inc(hf_ready, 1)

                if moe0:
                    split_high(0, 0)
                over_experts(act, body)

            @block.gpsimd
            def _(pool):
                def split_low(e, i):
                    pool.wait_ge(w_hi, e + 1)
                    pool.tensor_tensor(w1_lo[i][:, :, :], raw1[:, :, :], w1_hi[i][:, :, :].bitcast(F32), ALU.subtract)
                    pool.tensor_tensor(w2_lo[i][:, :, :], raw2[:, :, :], w2_hi[i][:, :, :].bitcast(F32), ALU.subtract)
                    pool.drain().then_inc(w_ready, 1)

                def body(e, i, last):
                    if not moe0:
                        split_low(e, i)
                    for tb in range(NB):
                        for j in range(NU):
                            cols = slice(j * 512, (j + 1) * 512)
                            pool.wait_ge(hf_ready, (e * NB + tb) * NU + j + 1 + U0)
                            pool.tensor_tensor(h_lo[tb % 2][:, cols], hf[:, tb % 2, j, :], h_hi[tb % 2][:, cols].bitcast(F32), ALU.subtract).then_inc(h_ready, 1)
                        if moe0 and tb == 1 and not last:
                            split_low(e + 1, 1 - i)

                if moe0:
                    split_low(0, 0)
                over_experts(pool, body)

            @block.vector
            def _(dve):
                for q, k in ((w_used, R), (y_free, 2), (y_ready, 2), (hf_ready, U0), (w_ready, 1)):
                    dve.sem_inc(q, k)

                def form(e, tb):
                    dve.wait_ge(y_ready, e * NB + tb + 1)
                    dve.wait_ge(sg_ready, e * NB + tb + 1)
                    up = bank[2 * (tb % 2) + 1]
                    dve.tensor_tensor(hf[:, tb % 2, 0, :], sg[:, tb % 2, :], up[:, :], ALU.mult)
                    dve.tensor_tensor(h_hi[tb % 2][:, :], sg[:, tb % 2, :], up[:, :], ALU.mult).then_inc(hf_ready, 1)

                def add(e, tb):
                    dve.wait_ge(y_ready, e * NB + tb + 3)
                    for t in range(TY):
                        tile = tb * TY + t
                        dve.scalar_tensor_tensor(x_res[:, tile, :], y_ps[tb % 2][:, t, :], gate[:, tile, bass.ds(e, 1)], x_res[:, tile, :], ALU.mult, ALU.add)
                    dve.drain().then_inc(y_free, 1)

                def body(e, i, last):
                    for tb in range(NB):
                        if moe0:
                            form(e, tb)
                            if tb >= 1:
                                add(e, tb - 1)
                            elif not (isinstance(e, int) and e == 0):
                                add(e - 1, NB - 1)
                        else:
                            add(e, tb)
                    if last:
                        add(e, NB - 1)

                over_experts(dve, body)


def build(nc, ins, out, stages=STAGES):
    with ExitStack() as ctx:
        x_res = ctx.enter_context(nc.sbuf_tensor("x_res", [P, TILES + TT, D], F32))
        pad_set = nc.alloc_semaphore(name="pad_set")
        ident = ctx.enter_context(nc.sbuf_tensor("ident", [P, P], F32))
        x_in = nc.alloc_semaphore(name="x_in")
        x_out = nc.alloc_semaphore(name="x_out")
        with nc.Block() as block:
            @block.sync
            def _(sp):
                sp.dma_start(ident[:, :], ins["ident"]).then_inc(x_in, 16)
                sp.dma_start(x_res[:, 0:TILES, :], ins["x"].rearrange("b (t p) d -> p (b t) d", p=P)).then_inc(x_in, 16)
                sp.wait_ge(x_in, 32)

            @block.gpsimd
            def _(pool):
                pool.memset(x_res[:, TILES:, :], 0.0).then_inc(pad_set, 1)
                pool.wait_ge(pad_set, 1)
        phases = ["L0_attn", "L0_xattn", "L0_ffn", "L1_attn", "L1_xattn", "L1_ffn"]
        for name in phases[:stages]:
            part = {k[len(name) + 1:]: v for k, v in ins.items() if k.startswith(name + "_")}
            if name in ATTN:
                attention_phase(nc, ATTN[name], x_res, ident, part)
            else:
                expert_phase(nc, name, x_res, ident, part)
        with nc.Block() as block:
            @block.sync
            def _(sp):
                sp.dma_start(out.rearrange("b (t p) d -> p (b t) d", p=P), x_res[:, 0:TILES, :]).then_inc(x_out, 16)
                sp.wait_ge(x_out, 16)

def layout(inputs):
    import numpy as np

    bf = mybir.dt.np(BF16)
    g = {k: np.asarray(v) for k, v in inputs.items()}
    a = {"ident": np.eye(P, dtype=np.float32), "x": g["x"]}

    def by_rows(wt):
        return wt.reshape(-1, P, wt.shape[1]).transpose(1, 0, 2)

    def column(v):
        return v.reshape(-1, P).T

    zeros = np.zeros(D, np.float32)
    for name, c in ATTN.items():
        w = {k: g.get(f"{name}_{k}") for k in ("Wq", "Wk", "Wv", "Wo", "bq", "bk", "bv", "bo", "Wgk", "bgk", "Wgv", "bgv")}
        for k in ("bq", "bk", "bv", "bo"):
            if w[k] is None:
                w[k] = zeros
        put = {}
        for k in "qkv":
            put["w" + k] = by_rows(w["W" + k].T)
        put["bq"], put["bk"] = column(w["bq"]), column(w["bk"])
        put["bv"], put["bo"] = np.broadcast_to(w["bv"], (P, c.inner)), np.broadcast_to(w["bo"], (P, D))
        wo = np.zeros((c.chunks, c.hpc, c.m, D), np.float32)
        wo[:, :, :c.dk, :] = w["Wo"].T.reshape(c.chunks, c.hpc, c.dk, D)
        put["wo"] = wo.reshape(c.chunks, P, D).transpose(1, 0, 2)
        if c.rope:
            half = c.dk // 2
            swap = np.arange(D).reshape(H, 2, half)[:, ::-1, :].reshape(-1)
            for k in "qk":
                put[f"w{k}r"] = by_rows(w["W" + k][swap].T)
                put[f"b{k}r"] = column(w["b" + k][swap])
            theta = 1.0 / 10000.0 ** (np.arange(0, c.dk, 2, dtype=np.float32) / np.float32(c.dk))
            theta = theta.astype(np.float32)
            ang = np.arange(1, S + 1, dtype=np.float32)[:, None] * theta[None, :]
            ang = np.concatenate([ang, ang], -1)
            sign = np.concatenate([-np.ones(half), np.ones(half)]).astype(np.float32)
            put["cos"] = np.tile(np.cos(ang).astype(np.float32).T, (P // c.dk, 1))
            put["sin"] = np.tile((np.sin(ang).astype(np.float32) * sign).T, (P // c.dk, 1))
        if c.wide:
            put["wgk"], put["wgv"] = by_rows(w["Wgk"].T), by_rows(w["Wgv"].T)
            put["bgk"], put["bgv"] = column(w["bgk"]), np.broadcast_to(w["bgv"], (P, c.inner))
            put["low_ident"] = (np.eye(P) * LOW).astype(bf)
            put["mask"] = g["mask_Bx16xSxS_bk1"]
            put["src"], put["grid"] = g["fside_BxSxS_0"], g["ctx_1024"]
        else:
            put["headmask"] = (np.arange(P)[:, None] // c.dk == np.arange(8)[None, :]).astype(np.float32)
        if c.causal:
            put["ident_bf"] = np.eye(P).astype(bf)
            put["tri"] = np.where(np.arange(P)[:, None] >= np.arange(P)[None, :], 0.0, LOW).astype(bf)
        if c.keymask:
            rest, parts = MASKED, []
            for _ in range(3):
                parts.append(np.asarray(rest).astype(bf))
                rest = rest - float(parts[-1])
            put["masked3"] = np.zeros((P, P), bf)
            put["masked3"][:3] = np.array(parts)[:, None]
            put["mask"] = g["mask_Bx1x1xS2_ik0"].reshape(B, S)
            put["src"] = g["ctx_1024"]
        a.update({f"{name}_{k}": v for k, v in put.items()})
    lower = np.broadcast_to((np.arange(8)[None, :] < np.arange(8)[:, None]).astype(np.float32), (P, 8, 8))
    a.update({
        "L0_ffn_wr": by_rows(g["L0_ffn_w_router"]), "L0_ffn_lower": lower, "L1_ffn_lower": lower,
        "L0_ffn_br": np.broadcast_to(g["L0_ffn_b_router"], (P, 64)),
        "L0_ffn_w_gate": g["L0_ffn_we_gate"], "L0_ffn_w_up": g["L0_ffn_we_up"], "L0_ffn_w_down": g["L0_ffn_we_down"],
        "L0_ffn_ws_gate": g["L0_ffn_ws_gate"], "L0_ffn_ws_up": g["L0_ffn_ws_up"], "L0_ffn_ws_down": g["L0_ffn_ws_down"],
        "L1_ffn_wr": by_rows(g["L1_ffn_gate_w"].T),
        "L1_ffn_w1": g["L1_ffn_w1"].transpose(0, 2, 1), "L1_ffn_w2": g["L1_ffn_w2"].transpose(0, 2, 1),
    })
    return {k: np.ascontiguousarray(v) for k, v in a.items()}

def kernel(**inputs):
    import numpy as np
    import concourse.bacc as bacc
    from concourse.bass_utils import run_bass_kernel_spmd

    nc = bacc.Bacc("TRN2", target_bir_lowering=False, num_devices=1)
    arrays = {f"in_{k}": v for k, v in layout(inputs).items()}
    aps = {k[3:]: nc.dram_tensor(k, v.shape, mybir.dt.from_np(v.dtype), kind="ExternalInput").ap() for k, v in arrays.items()}
    out = nc.dram_tensor("out", (B, S, D), F32, kind="ExternalOutput").ap()
    build(nc, aps, out)
    r = run_bass_kernel_spmd(nc, [arrays], core_ids=[0])
    return r.results[0]["out"]
```
